# Optimizing a Trainium2 kernel written in Bass

```python
import numpy as np
import jax
import jax.numpy as jnp

def _softmax(x, axis=-1):
    return jax.nn.softmax(x, axis=axis)

def _gelu(x):
    return jax.nn.gelu(x, approximate=True)

def _silu(x):
    return jax.nn.silu(x)

def _sigmoid(x):
    return jax.nn.sigmoid(x)

def _layernorm(x, axis=-1, eps=1e-05):
    m = jnp.mean(x, axis=axis, keepdims=True)
    v = jnp.var(x, axis=axis, keepdims=True)
    return (x - m) / jnp.sqrt(v + eps)

def _scatter_add(tgt, idx, src, axis=0):
    return tgt.at[idx].add(src)

def _segment_sum(src, seg, n):
    return jax.ops.segment_sum(src, seg, n)
kernel_name = 'mk_flamingo_gated_d1_seqx_r4_05d586'

def setup_inputs(seed: int=0):
    np.random.seed(seed)
    _w = jnp.asarray

    def _rec_inputs():
        import jax
        import jax.numpy as jnp
        _rk = jax.random.key(seed)
        x = -0.0002928 + 1 * jax.random.normal(jax.random.fold_in(_rk, 1), (16, 128, 256), jnp.float32)
        _lenS = 128 - jax.random.randint(jax.random.fold_in(_rk, 7), (16,), 0, max(1, 128 // 4) + 1, jnp.int32)
        _lenS2 = 128 - jax.random.randint(jax.random.fold_in(_rk, 8), (16,), 0, max(1, 128 // 4) + 1, jnp.int32)
        _ctx_1024P = jax.random.normal(jax.random.fold_in(_rk, 11), (16, 16, 256), jnp.float32)
        _ctx_1024c = jax.random.dirichlet(jax.random.fold_in(_rk, 511), 0.3 * jnp.ones((16,), jnp.float32), (16, 128))
        _ctx_1024t = jnp.einsum('bsk,bkd->bsd', _ctx_1024c, _ctx_1024P)
        _ctx_1024t = _ctx_1024t * jax.lax.rsqrt(jnp.mean(jnp.square(_ctx_1024t)) + 1e-12) * 0.953939
        ctx_1024 = -1.39393e-06 + 0.999914 * (_ctx_1024t + 0.3 * jax.random.normal(jax.random.fold_in(_rk, 611), (16, 128, 256), jnp.float32))
        fside_BxS2_0 = jax.random.uniform(jax.random.fold_in(_rk, 12), (16, 128), jnp.float32, 0.0, 0.499917)
        itok_BxS2_0_7 = jax.random.randint(jax.random.fold_in(_rk, 14), (16, 128), 0, 8, jnp.int32)
        _validS = jnp.arange(128)[None, :] < _lenS[:, None]
        _validS2 = jnp.arange(128)[None, :] < _lenS2[:, None]
        _causal = jnp.tril(jnp.ones((128, 128), dtype=bool))
        mask_BxS2_bf0 = jnp.logical_not(jnp.ones((16, 128), dtype=bool))
        _g = jax.random.normal(jax.random.fold_in(_rk, 9001), (2, 1), jnp.float32)
        _g = jnp.sign(_g) * jnp.maximum(jnp.abs(_g), 1.0) + (_g == 0) * 1.0
        g_xattn = _g[0]
        g_ffn = _g[1]
        return (x, ctx_1024, fside_BxS2_0, itok_BxS2_0_7, mask_BxS2_bf0, g_xattn, g_ffn)
    x, ctx_1024, fside_BxS2_0, itok_BxS2_0_7, mask_BxS2_bf0, g_xattn, g_ffn = _rec_inputs()

    def _L0_xattn_setup():
        import math
        import jax, jax.numpy as jnp
        import numpy as np
        D_MODEL = 256
        NUM_HEADS = 16
        N_BUCKETS = 8
        B, L, S = (2, 512, 512)
        NEG_INF = -1e+30
        key = jax.random.key(seed)
        ks = jax.random.split(key, 12)
        inv = 1.0 / math.sqrt(D_MODEL)
        return {'query': jax.random.normal(ks[0], (B, L, D_MODEL), jnp.float32), 'key': jax.random.normal(ks[1], (B, S, D_MODEL), jnp.float32), 'value': jax.random.normal(ks[2], (B, S, D_MODEL), jnp.float32), 'query_times': jax.random.uniform(ks[3], (B, L), jnp.float32) * 0.5, 'key_times': jax.random.uniform(ks[4], (B, S), jnp.float32), 'key_padding_mask': jnp.zeros((B, S), dtype=bool), 'source_bucket_ids': jax.random.randint(ks[5], (B, S), 0, N_BUCKETS, jnp.int32), 'Wq': jax.random.normal(ks[6], (D_MODEL, D_MODEL), jnp.float32) * inv, 'Wk_b': jax.random.normal(ks[7], (N_BUCKETS, D_MODEL, D_MODEL), jnp.float32) * inv, 'Wv_b': jax.random.normal(ks[8], (N_BUCKETS, D_MODEL, D_MODEL), jnp.float32) * inv, 'Wo': jax.random.normal(ks[9], (D_MODEL, D_MODEL), jnp.float32) * inv, 'bo': jnp.zeros((D_MODEL,), jnp.float32)}
    _L0_xattn_all = _L0_xattn_setup()
    _L0_xattn_in = {k: v for k, v in _L0_xattn_all.items() if k in ('Wq', 'Wk_b', 'Wv_b', 'Wo', 'bo')}
    del _L0_xattn_all

    def _L0_ffn_setup():
        import math
        import jax, jax.numpy as jnp
        import numpy as np
        B, T, D = (4, 1024, 256)
        H = 16
        HD = D // H
        CAP = int(1024 * 0.125)
        DFF = int(D * 4 * 2 / 3)
        EPS = 1e-06

        def rmsnorm(x, g):
            return x * jax.lax.rsqrt(jnp.mean(x * x, axis=-1, keepdims=True) + EPS) * g
        key = jax.random.key(seed)
        ks = jax.random.split(key, 9)
        s = lambda k, shape: jax.random.normal(k, shape, jnp.float32) * 0.02
        return {'x': jax.random.normal(ks[0], (B, T, D), jnp.float32), 'w_router': s(ks[1], (D,)), 'W_qkv': s(ks[2], (3 * D, D)), 'W_out': s(ks[3], (D, D)), 'g1': jnp.ones((D,), jnp.float32), 'g2': jnp.ones((D,), jnp.float32), 'W1': s(ks[4], (DFF, D)), 'W2': s(ks[5], (DFF, D)), 'W3': s(ks[6], (D, DFF))}
    _L0_ffn_all = _L0_ffn_setup()
    _L0_ffn_in = {k: v for k, v in _L0_ffn_all.items() if k in ('w_router', 'W_qkv', 'W_out', 'g1', 'g2', 'W1', 'W2', 'W3')}
    del _L0_ffn_all
    return {'x': x, 'ctx_1024': ctx_1024, 'fside_BxS2_0': fside_BxS2_0, 'itok_BxS2_0_7': itok_BxS2_0_7, 'mask_BxS2_bf0': mask_BxS2_bf0, 'g_xattn': g_xattn, 'g_ffn': g_ffn, 'L0_xattn_Wq': _L0_xattn_in['Wq'], 'L0_xattn_Wk_b': _L0_xattn_in['Wk_b'], 'L0_xattn_Wv_b': _L0_xattn_in['Wv_b'], 'L0_xattn_Wo': _L0_xattn_in['Wo'], 'L0_xattn_bo': _L0_xattn_in['bo'], 'L0_ffn_w_router': _L0_ffn_in['w_router'], 'L0_ffn_W_qkv': _L0_ffn_in['W_qkv'], 'L0_ffn_W_out': _L0_ffn_in['W_out'], 'L0_ffn_g1': _L0_ffn_in['g1'], 'L0_ffn_g2': _L0_ffn_in['g2'], 'L0_ffn_W1': _L0_ffn_in['W1'], 'L0_ffn_W2': _L0_ffn_in['W2'], 'L0_ffn_W3': _L0_ffn_in['W3']}

def reference(x, ctx_1024, fside_BxS2_0, itok_BxS2_0_7, mask_BxS2_bf0, g_xattn, g_ffn, L0_xattn_Wq, L0_xattn_Wk_b, L0_xattn_Wv_b, L0_xattn_Wo, L0_xattn_bo, L0_ffn_w_router, L0_ffn_W_qkv, L0_ffn_W_out, L0_ffn_g1, L0_ffn_g2, L0_ffn_W1, L0_ffn_W2, L0_ffn_W3):
    import jax
    import jax.numpy as jnp

    def _L0_xattn_ref(query, key, value, query_times, key_times, key_padding_mask, source_bucket_ids, Wq, Wk_b, Wv_b, Wo, bo):
        import math
        import jax, jax.numpy as jnp
        import numpy as np
        D_MODEL = 256
        NUM_HEADS = 16
        N_BUCKETS = 8
        B, L, S = (2, 512, 512)
        NEG_INF = -1e+30
        Bq, Lq, D = query.shape
        Sq = key.shape[1]
        H = NUM_HEADS
        dk = D // H
        Q = (query @ Wq).reshape(Bq, Lq, H, dk).transpose(0, 2, 1, 3)
        N = Bq * Sq
        kf = key.reshape(N, D)
        vf = value.reshape(N, D)
        buckets = source_bucket_ids.reshape(N)
        K_all = jnp.einsum('nd,edk->enk', kf, Wk_b)
        V_all = jnp.einsum('nd,edk->enk', vf, Wv_b)
        rows = jnp.arange(N)
        Kf = K_all[buckets, rows]
        Vf = V_all[buckets, rows]
        K = Kf.reshape(Bq, Sq, H, dk).transpose(0, 2, 1, 3)
        V = Vf.reshape(Bq, Sq, H, dk).transpose(0, 2, 1, 3)
        time_diff = query_times[:, :, None] - key_times[:, None, :]
        attend = (time_diff < 0)[:, None, :, :] | key_padding_mask[:, None, None, :]
        scores = jnp.einsum('bhld,bhsd->bhls', Q, K) / math.sqrt(dk)
        scores = jnp.where(attend, scores, NEG_INF)
        attn = jax.nn.softmax(scores, axis=-1)
        ctx = jnp.einsum('bhls,bhsd->bhld', attn, V)
        ctx = ctx.transpose(0, 2, 1, 3).reshape(Bq, Lq, D)
        return ctx @ Wo + bo

    def _L0_ffn_ref(x, w_router, W_qkv, W_out, g1, g2, W1, W2, W3):
        import math
        import jax, jax.numpy as jnp
        import numpy as np
        B, T, D = (4, 1024, 256)
        H = 16
        HD = D // H
        CAP = int(1024 * 0.125)
        DFF = int(D * 4 * 2 / 3)
        EPS = 1e-06

        def rmsnorm(x, g):
            return x * jax.lax.rsqrt(jnp.mean(x * x, axis=-1, keepdims=True) + EPS) * g
        Bq, Tq, Dq = x.shape
        scores = x @ w_router
        _, idx = jax.lax.top_k(scores, CAP)
        x_sel = jnp.take_along_axis(x, idx[:, :, None], axis=1)
        h = rmsnorm(x_sel, g1)
        qkv = (h @ W_qkv.T).reshape(Bq, CAP, 3, H, HD)
        q, k, v = jnp.moveaxis(qkv, 2, 0)
        att = jnp.einsum('bqhd,bkhd->bhqk', q, k) / math.sqrt(HD)
        mask = jnp.triu(jnp.ones((CAP, CAP), bool), 1)
        att = jnp.where(mask, -jnp.inf, att)
        att = jax.nn.softmax(att, axis=-1)
        o = jnp.einsum('bhqk,bkhd->bqhd', att, v).reshape(Bq, CAP, Dq)
        x_attn = o @ W_out.T
        h2 = rmsnorm(x_sel + x_attn, g2)
        x_ff = jax.nn.silu(h2 @ W1.T) * (h2 @ W2.T) @ W3.T
        x_proc = x_sel + x_attn + x_ff
        out = x.at[jnp.arange(Bq)[:, None], idx].set(x_proc)
        return out
    x = x + jnp.tanh(g_xattn[0]) * _L0_xattn_ref(_layernorm(x, axis=-1), ctx_1024, ctx_1024, fside_BxS2_0, fside_BxS2_0, mask_BxS2_bf0, itok_BxS2_0_7, L0_xattn_Wq, L0_xattn_Wk_b, L0_xattn_Wv_b, L0_xattn_Wo, L0_xattn_bo)
    x = x + jnp.tanh(g_ffn[0]) * _L0_ffn_ref(_layernorm(x, axis=-1), L0_ffn_w_router, L0_ffn_W_qkv, L0_ffn_W_out, L0_ffn_g1, L0_ffn_g2, L0_ffn_W1, L0_ffn_W2, L0_ffn_W3)
    return x

_drawn_inputs = setup_inputs


def setup_inputs(seed=0):
    import zlib

    import numpy as np

    out = dict(_drawn_inputs(seed))
    spreads = {'L0_xattn_bo': (0.0, 0.1), 'L0_ffn_g1': (1.0, 0.2), 'L0_ffn_g2': (1.0, 0.2)}
    factors = {}
    for name, (base, spread) in spreads.items():
        noise = np.random.default_rng([zlib.crc32(name.encode()), seed]).standard_normal(out[name].shape)
        drawn = base * np.exp(spread * noise) if base else spread * noise
        out[name] = jnp.asarray(drawn.astype(out[name].dtype))
    for name, factor in factors.items():
        out[name] = (out[name] * factor).astype(out[name].dtype)
    return out
```

```python
import numpy as np
import concourse.bass as bass
from concourse import mybir
from contextlib import ExitStack

F32 = mybir.dt.float32
BF16 = mybir.dt.bfloat16
I32 = mybir.dt.int32
U32 = mybir.dt.uint32
U8 = mybir.dt.uint8
ALU = mybir.AluOpType
ACT = mybir.ActivationFunctionType
AX = mybir.AxisListType

P = 128
B = 16
D = 256
KC = D // P
H = 16
HD = D // H
G = 4
C = H // G
SLOT = P // G
E = 8
NTILE = B + E
DFF = 682
FC = 6
DFFP = FC * P
NEG = -float(2 ** 100)
SCALE = 1.0 / float(HD) ** 0.5
LN_EPS = 1e-5
RMS_EPS = 1e-6
NS = 2
NB = B // NS
UN = 4


def build(nc, x, ctx_in, times, times_t, bucket_t, pad, pad_t, g_x, g_f, wq, wkv, wo, bo,
          w_router, wqkv_t, wout_t, g1, g2, w1t, w2t, w3t, out):
    stack = ExitStack()
    with stack:
        def sb(name, shape, dt=F32):
            return stack.enter_context(nc.sbuf_tensor(name, shape, dt))

        def pair(name, shape, dt=F32):
            return [sb(f"{name}{s}", shape, dt) for s in range(NS)]

        def sem(name):
            return stack.enter_context(nc.semaphore(name))

        def sems(name, n=NS):
            return [sem(f"{name}{s}") for s in range(n)]

        token_of_slot = nc.dram_tensor("token_of_slot", [NTILE * P, 1], F32, kind="Internal").ap()
        kv_sorted = nc.dram_tensor("kv_sorted", [NTILE * P, 2 * D], F32, kind="Internal").ap()

        ident = sb("ident", [P, P])
        ident_b = sb("ident_b", [P, P], BF16)
        ones_b = sb("ones_b", [P, P], BF16)
        before_b = sb("before_b", [P, P], BF16)
        later_neg = sb("later_neg", [P, P])
        earlier_neg = sb("earlier_neg", [P, P])
        neg_half = sb("neg_half", [P, 2])
        pool_held = sb("pool_held", [1, 1])
        dve_held = sb("dve_held", [1, 1])
        minus_one_rows = sb("minus_one_rows", [P, 1])
        tile_marks = sb("tile_marks", [P, B])
        tile_ids = sb("tile_ids", [P, NTILE])
        token_ids_i = sb("token_ids_i", [P, B], I32)
        token_ids = sb("token_ids", [P, B])
        scan_keep = sb("scan_keep", [P, E, B])
        ones_e = sb("ones_e", [P, E])
        wkv_sb = sb("wkv_sb", [P, KC, E, 2 * D])
        raw_q = sb("raw_q", [P, KC, D])
        wq_pad = sb("wq_pad", [P, KC, H * SLOT])
        wo_sb = sb("wo_sb", [P, KC, D])
        raw_qkv = sb("raw_qkv", [P, KC, 3 * D])
        wq2_pad = sb("wq2_pad", [P, KC, H * SLOT])
        wk2_pad = sb("wk2_pad", [P, KC, H * SLOT])
        wv2 = sb("wv2", [P, KC, D])
        wout_sb = sb("wout_sb", [P, KC, D])
        raw_ff = sb("raw_ff", [P, 2, KC, DFF])
        w1_pad = sb("w1_pad", [P, KC, DFFP])
        w2_pad = sb("w2_pad", [P, KC, DFFP])
        w3_pad = sb("w3_pad", [P, FC, D])
        g1_col = sb("g1_col", [P, KC])
        g2_col = sb("g2_col", [P, KC])
        router_row = sb("router_row", [P, D])
        bias_row = sb("bias_row", [P, D])
        gates = sb("gates", [P, 2])
        gates_raw = sb("gates_raw", [P, 2])
        time_rows = sb("time_rows", [P, B * P])
        time_cols = sb("time_cols", [P, B])
        pad_rows = sb("pad_rows", [P, B * P], U8)
        pad_cols = sb("pad_cols", [P, B], U8)
        open_rows = sb("open_rows", [P, B * P], BF16)
        open_cols = sb("open_cols", [P, B])

        bucket_i = sb("bucket_i", [P, B], I32)
        onehot = sb("onehot", [P, E, B])
        onehot_b = sb("onehot_b", [P, E, B], BF16)
        totals_scan = sb("totals_scan", [P, E, B])
        rank = sb("rank", [P, E, B])
        over = sb("over", [P, E, B])
        tiles_e = sb("tiles_e", [P, E])
        tiles_end = sb("tiles_end", [P, E])
        tiles_base = sb("tiles_base", [P, E])
        slot_f = sb("slot_f", [P, B])
        slot_u = sb("slot_u", [P, B], U32)
        past = sb("past", [1, NTILE, E])
        expert_f = sb("expert_f", [1, NTILE])
        expert_i = sb("expert_i", [1, NTILE], I32)
        table_zero = sb("table_zero", [NTILE, P])
        table_rows = sb("table_rows", [NTILE, P])
        table_cols = sb("table_cols", [P, NTILE], U32)
        tile_index = sb("tile_index", [P, UN], U32)
        tile_ctx = [sb(f"tile_ctx{j}", [P, D]) for j in range(UN)]
        tile_ctx_t = [sb(f"tile_ctx_t{j}", [P, KC, P]) for j in range(2)]
        tile_kv = [sb(f"tile_kv{j}", [P, 2 * D]) for j in range(UN)]

        x_sb = pair("x_sb", [P, D])
        kv_index = pair("kv_index", [P, 1], U32)
        kv_raw = pair("kv_raw", [P, 2 * D])
        k_pad = pair("k_pad", [P, H, SLOT])
        v1 = pair("v1", [P, H, HD + 1])
        v2 = pair("v2", [P, H, HD + 1])
        x_bias = pair("x_bias", [P, D])
        stats = pair("stats", [P, 6])
        mean_var = pair("mean_var", [P, 2])
        pow_in = pair("pow_in", [P, 2])
        pow_out = pair("pow_out", [P, 2])
        any_open = pair("any_open", [P, 1])
        q_rstd = pair("q_rstd", [P, 1])
        neg_l = pair("neg_l", [P, P], BF16)
        neg_t = pair("neg_t", [P, P], BF16)
        mask_a = pair("mask_a", [P, P])
        mask_b = pair("mask_b", [P, P])
        xn = pair("xn", [P, D])
        xn_t = pair("xn_t", [P, KC, P])
        q_t = pair("q_t", [P, C, P])
        k_t = pair("k_t", [P, C, P])
        q_aug = pair("q_aug", [P, C, P])
        max_pad = pair("max_pad", [P, C, G, SLOT])
        probs = pair("probs", [P, G, C, P])
        denom = pair("denom", [P, H])
        attn = pair("attn", [P, D])
        attn_t = pair("attn_t", [P, KC, P])
        x1 = pair("x1", [P, D])
        y = pair("y", [P, D])
        junk = pair("junk", [P, D])
        score = pair("score", [P, 1])
        score_wide = pair("score_wide", [P, P])
        h = pair("h", [P, D])
        h_t = pair("h_t", [P, KC, P])
        x2 = pair("x2", [P, D])
        h2 = pair("h2", [P, D])
        h2_t = pair("h2_t", [P, KC, P])
        probs_flat = [t[:, :, :, :].rearrange("p g c m -> p (g c m)") for t in probs]
        tanh_a = [t[:, 0:DFFP] for t in probs_flat]
        silu_a = tanh_a
        hidden = [t[:, DFFP:2 * DFFP] for t in probs_flat]
        x3 = pair("x3", [P, D])
        y_out = pair("y_out", [P, D])

        banks = [stack.enter_context(nc.psum_tensor(f"bank{i}", [P, 512], F32)) for i in range(8)]

        def bank(s, g):
            return banks[4 * s + g]

        bucket_loaded = sem("bucket_loaded")
        small_loaded = sem("small_loaded")
        rows_loaded = sem("rows_loaded")
        weights_loaded = sem("weights_loaded")
        wkv_loaded = sem("wkv_loaded")
        pool_const = sem("pool_const")
        pool_step = sem("pool_step")
        pool_carried = sem("pool_carried")
        consts_ready = sem("consts_ready")
        dve_const = sem("dve_const")
        weights_ready = sem("weights_ready")
        route = sem("route")
        onehot_ready = sem("onehot_ready")
        counts_ready = sem("counts_ready")
        slots_ready = sem("slots_ready")
        experts_ready = sem("experts_ready")
        gates_ready = sem("gates_ready")
        table_zeroed = sem("table_zeroed")
        table_filled = sem("table_filled")
        table_loaded = sem("table_loaded")
        table_turned = sem("table_turned")
        table_ready = sem("table_ready")
        index_ready = sem("index_ready")
        ctx_gathered = sems("ctx_gathered", UN)
        ctx_turned = sems("ctx_turned", UN)
        ctx_t_ready = sems("ctx_t_ready", UN)
        kv_in_psum = sems("kv_in_psum", UN)
        kv_copied = sems("kv_copied", UN)
        kv_stored = sems("kv_stored", UN)

        x_loaded = sems("x_loaded")
        kv_index_ready = sems("kv_index_ready")
        kv_gathered = sems("kv_gathered")
        k_pad_ready = sems("k_pad_ready")
        v1_ready = sems("v1_ready")
        v2_ready = sems("v2_ready")
        x_bias_ready = sems("x_bias_ready")
        dve_step = sems("dve_step")
        pow_asked = sems("pow_asked")
        pow_ready = sems("pow_ready")
        masks_ready = sems("masks_ready")
        xn_ready = sems("xn_ready")
        xn_in_psum = sems("xn_in_psum")
        xn_t_ready = sems("xn_t_ready")
        q_in_psum = sems("q_in_psum")
        k_in_psum = sems("k_in_psum")
        v_in_psum = sems("v_in_psum")
        q_t_ready = sems("q_t_ready")
        k_t_ready = sems("k_t_ready")
        scores_ready = sems("scores_ready")
        max_ready = sems("max_ready")
        max_in_psum = sems("max_in_psum")
        q_aug_ready = sems("q_aug_ready")
        scores_t_ready = sems("scores_t_ready")
        probs_ready = sems("probs_ready")
        pv_ready = sems("pv_ready")
        attn_ready = sems("attn_ready")
        attn_in_psum = sems("attn_in_psum")
        attn_t_ready = sems("attn_t_ready")
        mixed_ready = sems("mixed_ready")
        score_ready = sems("score_ready")
        score_in_psum = sems("score_in_psum")
        h_ready = sems("h_ready")
        h_in_psum = sems("h_in_psum")
        h_t_ready = sems("h_t_ready")
        h2_ready = sems("h2_ready")
        h2_in_psum = sems("h2_in_psum")
        h2_t_ready = sems("h2_t_ready")
        ff_a_ready = sems("ff_a_ready")
        ff_b_ready = sems("ff_b_ready")
        tanh_ready = sems("tanh_ready")
        hidden_ready = sems("hidden_ready")
        ff_ready = sems("ff_ready")
        out_ready = sems("out_ready")
        out_stored = sems("out_stored")

        block = stack.enter_context(nc.Block())

        @block.sync
        def _(sp):
            sp.dma_start(bucket_i[:, :], bucket_t).then_inc(bucket_loaded, 16)
            sp.dma_start(wkv_sb[:, :, :, :].rearrange("p a e n -> p (a e n)"), wkv).then_inc(wkv_loaded, 16)
            sp.wait_ge(table_filled, 16 * B)
            sp.dma_start(table_rows[:, :], token_of_slot.rearrange("(t m) o -> t (m o)", m=P)).then_inc(table_loaded, 16)

            def load_x(s, it):
                sp.dma_start(x_sb[s][:, :], x[bass.ds(NS * it + s, 1), :, :].rearrange("a p d -> (a p) d")
                             ).then_inc(x_loaded[s], 16)

            for s in range(NS):
                load_x(s, 0)
            with sp.Fori(0, NTILE // UN) as i:
                for j in range(UN):
                    sp.wait_ge(kv_copied[j], i + 1)
                    sp.dma_start(kv_sorted[bass.ds((UN * i + j) * P, P), :], tile_kv[j][:, :]).then_inc(kv_stored[j], 16)

            def next_loads_and_store(it, more):
                for s in range(NS):
                    if more:
                        sp.wait_ge(x_bias_ready[s], it + 1)
                        sp.wait_ge(xn_ready[s], it + 1)
                        load_x(s, it + 1)
                for s in range(NS):
                    sp.wait_ge(out_ready[s], it + 1)
                    sp.dma_start(out[bass.ds(NS * it + s, 1), :, :].rearrange("a p d -> (a p) d"), y_out[s][:, :]
                                 ).then_inc(out_stored[s], 16)

            with sp.Fori(0, NB - 1) as it:
                next_loads_and_store(it, True)
            next_loads_and_store(NB - 1, False)
            for s in range(NS):
                sp.wait_ge(out_stored[s], 16 * NB)
            for j in range(UN):
                sp.wait_ge(kv_stored[j], 16 * (NTILE // UN))

        @block.gpsimd
        def _(pool):
            pool.memset(table_zero[:, :], 0.0).then_inc(pool_step, 1)
            pool.memset(ident[:, :], 0.0).then_inc(pool_const, 1)
            pool.memset(before_b[:, :], 1.0).then_inc(pool_const, 1)
            pool.memset(later_neg[:, :], NEG).then_inc(pool_const, 1)
            pool.memset(earlier_neg[:, :], NEG).then_inc(pool_const, 1)
            pool.memset(minus_one_rows[:, :], 0.0).then_inc(pool_const, 1)
            pool.memset(scan_keep[:, :, :], 1.0).then_inc(pool_const, 1)
            pool.iota(token_ids_i[:, :], pattern=[[P, B]], base=0, channel_multiplier=1).then_inc(pool_const, 1)
            pool.memset(ones_b[:, :], 1.0)
            pool.memset(ones_e[:, :], 1.0)
            pool.memset(neg_half[:, :], -0.5)
            pool.wait_ge(pool_step, 1)
            pool.dma_start(token_of_slot.rearrange("(t m) o -> t (m o)", m=P), table_zero[:, :]).then_inc(table_zeroed, 16)
            pool.wait_ge(pool_const, 7)
            pool.affine_select(out=ident[:, :], in_=ident[:, :], compare_op=ALU.not_equal, fill=1.0,
                               base=0, pattern=[[-1, P]], channel_multiplier=1).then_inc(pool_const, 1)
            pool.affine_select(out=before_b[:, :], in_=before_b[:, :], compare_op=ALU.is_gt, fill=0.0,
                               base=0, pattern=[[1, P]], channel_multiplier=-1)
            pool.affine_select(out=later_neg[:, :], in_=later_neg[:, :], compare_op=ALU.is_gt, fill=0.0,
                               base=0, pattern=[[1, P]], channel_multiplier=-1)
            pool.affine_select(out=earlier_neg[:, :], in_=earlier_neg[:, :], compare_op=ALU.is_gt, fill=0.0,
                               base=0, pattern=[[-1, P]], channel_multiplier=1)
            pool.affine_select(out=scan_keep[:, :, :], in_=scan_keep[:, :, :], compare_op=ALU.not_equal, fill=0.0,
                               base=0, pattern=[[0, E], [1, B]], channel_multiplier=0)
            for g in range(G):
                ins = pool.affine_select(out=minus_one_rows[:, :], in_=minus_one_rows[:, :], compare_op=ALU.not_equal,
                                         fill=-1.0, base=-(SLOT * g + HD), pattern=[[0, 1]], channel_multiplier=1)
                ins.then_inc(pool_const, 1)
                pool.wait_ge(pool_const, 9 + g)
            pool.tensor_copy(token_ids[:, :], token_ids_i[:, :])
            pool.iota(tile_marks[:, :], pattern=[[P, B]], base=0, channel_multiplier=0,
                      allow_small_or_imprecise_dtypes=True)
            pool.iota(tile_ids[:, :], pattern=[[1, NTILE]], base=0, channel_multiplier=0,
                      allow_small_or_imprecise_dtypes=True)
            pool.tensor_copy(ident_b[:, :], ident[:, :]).then_inc(consts_ready, 1)
            pool.wait_ge(consts_ready, 1)
            pool.wait_ge(table_zeroed, 16)
            pool.wait_ge(slots_ready, 1)
            for b in range(B):
                pool.indirect_dma_start(out=token_of_slot, out_offset=bass.IndirectOffsetOnAxis(ap=slot_u[:, b:b + 1], axis=0),
                                        in_=token_ids[:, b:b + 1], in_offset=None).then_inc(table_filled, 16)
            for s in range(NS):
                pool.memset(k_pad[s][:, :, :], 0.0)
                pool.memset(v1[s][:, :, :], 1.0)
                pool.memset(v2[s][:, :, :], 1.0)
                pool.memset(max_pad[s][:, :, :, :], 0.0).then_inc(consts_ready, 1)
            pool.wait_ge(consts_ready, 1 + NS)
            pool.wait_ge(table_ready, 1)
            def hold():
                pool.wait_ge(table_ready, 1)

            def carry(n):
                pool.wait_ge(pool_carried, n)
                pool.tensor_tensor(pool_held[:, :], neg_half[0:1, 0:1], neg_half[0:1, 0:1], ALU.add).then_inc(pool_carried, 1)

            with pool.Fori(0, NTILE // UN) as i:
                hold()
                for j in range(UN):
                    pool.wait_ge(ctx_gathered[j], 16 * i)
                pool.tensor_copy(tile_index[:, :], table_cols[:, bass.ds(UN * i, UN)]).then_inc(index_ready, 1)
                for j in range(UN):
                    pool.wait_ge(index_ready, i + 1)
                    pool.wait_ge(ctx_turned[j], i)
                    carry(UN * i + j)
                    pool.indirect_dma_start(out=tile_ctx[j][:, :], out_offset=None, in_=ctx_in,
                                            in_offset=bass.IndirectOffsetOnAxis(ap=tile_index[:, j:j + 1], axis=0)
                                            ).then_inc(ctx_gathered[j], 16)

            def gather_kv(s, it):
                pool.tensor_copy(kv_index[s][:, :], slot_u[:, bass.ds(NS * it + s, 1)]).then_inc(kv_index_ready[s], 1)
                pool.wait_ge(kv_index_ready[s], it + 1)
                carry(NTILE + NS * it + s)
                pool.indirect_dma_start(out=kv_raw[s][:, :], out_offset=None, in_=kv_sorted,
                                        in_offset=bass.IndirectOffsetOnAxis(ap=kv_index[s][:, 0:1], axis=0)
                                        ).then_inc(kv_gathered[s], 16)

            def spread_kv(s, it):
                pool.tensor_copy(k_pad[s][:, :, 0:HD], kv_raw[s][:, 0:D].rearrange("p (h d) -> p h d", h=H)
                                 ).then_inc(k_pad_ready[s], 1)
                pool.tensor_copy(v1[s][:, :, 0:HD], kv_raw[s][:, D:2 * D].rearrange("p (h d) -> p h d", h=H)
                                 ).then_inc(v1_ready[s], 1)

            def add_bias(s, it):
                pool.wait_ge(x_loaded[s], 16 * it + 16)
                pool.wait_ge(mixed_ready[s], 2 * it)
                pool.tensor_tensor(x_bias[s][:, :], x_sb[s][:, :], bias_row[:, :], ALU.add).then_inc(x_bias_ready[s], 1)

            def power(s, it, k):
                pool.wait_ge(pow_asked[s], 3 * it + k + 1)
                if k == 0:
                    pool.wait_ge(kv_gathered[s], 16 * it + 16)
                    pool.wait_ge(k_in_psum[s], 2 * it)
                    pool.wait_ge(pv_ready[s], 2 * it)
                pool.tensor_tensor(pow_out[s][:, :], pow_in[s][:, :], neg_half[:, :], ALU.pow).then_inc(pow_ready[s], 1)

            for j in range(UN):
                pool.wait_ge(kv_stored[j], 16 * (NTILE // UN))
            for s in range(NS):
                gather_kv(s, 0)
            pool.wait_ge(weights_ready, 1)

            def rows(it, more):
                for s in range(NS):
                    power(s, it, 0)
                    spread_kv(s, it)
                    add_bias(s, it)
                for s in range(NS):
                    if more:
                        hold()
                        pool.wait_ge(v1_ready[s], it + 1)
                        gather_kv(s, it + 1)
                for s in range(NS):
                    power(s, it, 1)
                for s in range(NS):
                    power(s, it, 2)

            with pool.Fori(0, NB - 1) as it:
                rows(it, True)
            rows(NB - 1, False)

        @block.scalar
        def _(act):
            act.dma_start(gates_raw[:, 0:1], g_x.rearrange("(a n) -> a n", a=1).to_broadcast([P, 1])).then_inc(small_loaded, 16)
            act.dma_start(gates_raw[:, 1:2], g_f.rearrange("(a n) -> a n", a=1).to_broadcast([P, 1])).then_inc(small_loaded, 16)
            act.dma_start(g1_col[:, :], g1).then_inc(small_loaded, 16)
            act.dma_start(g2_col[:, :], g2).then_inc(small_loaded, 16)
            act.dma_start(time_cols[:, :], times_t).then_inc(small_loaded, 16)
            act.dma_start(pad_cols[:, :], pad_t).then_inc(small_loaded, 16)
            act.dma_start(router_row[:, :], w_router.rearrange("(a n) -> a n", a=1).to_broadcast([P, D])).then_inc(small_loaded, 16)
            act.dma_start(bias_row[:, :], bo.rearrange("(a n) -> a n", a=1).to_broadcast([P, D])).then_inc(small_loaded, 16)
            act.dma_start(time_rows[:, :], times.rearrange("(a b) t -> a (b t)", a=1).to_broadcast([P, B * P])).then_inc(rows_loaded, 16)
            act.dma_start(pad_rows[:, :], pad.rearrange("(a b) t -> a (b t)", a=1).to_broadcast([P, B * P])).then_inc(rows_loaded, 16)
            act.dma_start(raw_q[:, :, :], wq.rearrange("(k p) n -> p k n", p=P)).then_inc(weights_loaded, 16)
            act.dma_start(wo_sb[:, :, :], wo.rearrange("(k p) n -> p k n", p=P)).then_inc(weights_loaded, 16)
            act.dma_start(raw_qkv[:, :, :], wqkv_t.rearrange("(k p) n -> p k n", p=P)).then_inc(weights_loaded, 16)
            act.dma_start(wout_sb[:, :, :], wout_t.rearrange("(k p) n -> p k n", p=P)).then_inc(weights_loaded, 16)
            act.dma_start(raw_ff[:, 0, :, :], w1t.rearrange("(k p) n -> p k n", p=P)).then_inc(weights_loaded, 16)
            act.dma_start(raw_ff[:, 1, :, :], w2t.rearrange("(k p) n -> p k n", p=P)).then_inc(weights_loaded, 16)
            act.dma_start(w3_pad[:, 0:FC - 1, :], w3t[0:(FC - 1) * P, :].rearrange("(k p) n -> p k n", p=P)).then_inc(weights_loaded, 16)
            act.wait_ge(dve_const, 1)
            act.dma_start(w3_pad[0:DFF - (FC - 1) * P, FC - 1, :], w3t[(FC - 1) * P:DFF, :]).then_inc(weights_loaded, 16)
            act.wait_ge(small_loaded, 16 * 8)
            act.activation(gates[:, :], gates_raw[:, :], ACT.Tanh).then_inc(gates_ready, 1)

            with act.Fori(0, NTILE // UN) as i:
                for j in range(UN):
                    act.wait_ge(ctx_turned[j], i + 1)
                    act.activation(tile_ctx_t[j % 2][:, :, :], banks[j % 2][:, 0:D].rearrange("p (k m) -> p k m", k=KC),
                                   ACT.Copy).then_inc(ctx_t_ready[j], 1)

            def three(t):
                return t.rearrange("p (k m) -> p k m", k=KC)

            def copy_xn(s, it):
                act.wait_ge(xn_in_psum[s], it + 1)
                act.activation(xn_t[s][:, :, :], three(bank(s, 0)[:, 0:D]), ACT.Copy).then_inc(xn_t_ready[s], 1)

            def copy_qk(s, u):
                act.wait_ge(q_in_psum[s], u + 1)
                act.activation(q_t[s][:, :, :], bank(s, 1)[:, :].rearrange("p (c m) -> p c m", c=C),
                               ACT.Copy).then_inc(q_t_ready[s], 1)
                act.wait_ge(k_in_psum[s], u + 1)
                act.activation(k_t[s][:, :, :], bank(s, 2)[:, :].rearrange("p (c m) -> p c m", c=C),
                               ACT.Identity, bias=minus_one_rows[:, 0:1]).then_inc(k_t_ready[s], 1)

            def copy_v(s, it):
                act.wait_ge(v_in_psum[s], it + 1)
                act.activation(v2[s][:, :, 0:HD], bank(s, 3)[:, 0:D].rearrange("p (h d) -> p h d", h=H),
                               ACT.Copy).then_inc(v2_ready[s], 1)

            def exponentials(s, u):
                act.wait_ge(scores_t_ready[s], u + 1)
                for g in range(G):
                    act.activation(probs[s][:, g, :, :], bank(s, g)[:, :].rearrange("p (c m) -> p c m", c=C),
                                   ACT.Exp, scale=SCALE).then_inc(probs_ready[s], 1)

            def copy_attn(s, u):
                act.wait_ge(attn_in_psum[s], u + 1)
                act.activation(attn_t[s][:, :, :], three(bank(s, 1)[:, 0:D]), ACT.Copy).then_inc(attn_t_ready[s], 1)

            def copy_h(s, it):
                act.wait_ge(h_in_psum[s], it + 1)
                act.activation(h_t[s][:, :, :], three(bank(s, 3)[:, 0:D]), ACT.Copy).then_inc(h_t_ready[s], 1)

            def copy_h2(s, it):
                act.wait_ge(h2_in_psum[s], it + 1)
                act.activation(h2_t[s][:, :, :], three(bank(s, 0)[:, 0:D]), ACT.Copy).then_inc(h2_t_ready[s], 1)

            def tanh_half(s, it):
                act.wait_ge(ff_a_ready[s], it + 1)
                act.activation(tanh_a[s][:, 0:512], bank(s, 1)[:, :], ACT.Tanh, scale=0.5)
                act.activation(tanh_a[s][:, 512:DFFP], bank(s, 2)[:, 0:DFFP - 512], ACT.Tanh, scale=0.5
                               ).then_inc(tanh_ready[s], 1)

            with act.Fori(0, NB) as it:
                for s in range(NS):
                    copy_xn(s, it)
                for s in range(NS):
                    copy_qk(s, 2 * it)
                for s in range(NS):
                    exponentials(s, 2 * it)
                for s in range(NS):
                    copy_attn(s, 2 * it)
                for s in range(NS):
                    copy_h(s, it)
                for s in range(NS):
                    copy_qk(s, 2 * it + 1)
                    copy_v(s, it)
                for s in range(NS):
                    exponentials(s, 2 * it + 1)
                for s in range(NS):
                    copy_attn(s, 2 * it + 1)
                for s in range(NS):
                    copy_h2(s, it)
                for s in range(NS):
                    tanh_half(s, it)

        @block.tensor
        def _(pe):
            pe.wait_ge(consts_ready, 1)
            pe.wait_ge(onehot_ready, 1)
            pe.matmul(banks[6][:, 0:P], before_b[:, :], onehot_b[:, :, :], start=True, stop=True)
            pe.matmul(banks[7][:, 0:P], ones_b[:, :], onehot_b[:, :, :], start=True, stop=True).then_inc(counts_ready, 1)
            pe.wait_ge(table_loaded, 16)
            pe.transpose(banks[5][:, 0:NTILE], table_rows[:, :], ident[0:NTILE, 0:NTILE]).then_inc(table_turned, 1)

            def turn(dst, src):
                for k in range(KC):
                    ins = pe.transpose(dst[:, k * P:(k + 1) * P], src[:, k * P:(k + 1) * P], ident[:, :])
                return ins

            def turn_tile(j, i):
                pe.wait_ge(ctx_gathered[j], 16 * i + 16)
                turn(banks[j % 2], tile_ctx[j]).then_inc(ctx_turned[j], 1)

            def project_tile(j, i):
                expert = nc.tensor.value_load(expert_i[0:1, bass.ds(UN * i + j, 1)], min_val=0, max_val=E - 1)
                pe.wait_ge(ctx_t_ready[j], i + 1)
                pe.wait_ge(kv_copied[j], i)
                for k in range(KC):
                    ins = pe.matmul(banks[2 + j][:, :], tile_ctx_t[j % 2][:, k, :],
                                    wkv_sb[:, k, bass.ds(expert, 1), :].rearrange("p a n -> p (a n)"),
                                    start=(k == 0), stop=(k == KC - 1))
                ins.then_inc(kv_in_psum[j], 1)

            pe.wait_ge(wkv_loaded, 16)
            pe.wait_ge(experts_ready, 1)
            pe.wait_ge(table_ready, 1)
            with pe.Fori(0, NTILE // UN) as i:
                turn_tile(0, i)
                for j in range(UN):
                    if j + 1 < UN:
                        if j + 1 >= 2:
                            pe.wait_ge(ctx_t_ready[j - 1], i + 1)
                        turn_tile(j + 1, i)
                    project_tile(j, i)

            def turn_xn(s, it):
                pe.wait_ge(xn_ready[s], it + 1)
                turn(bank(s, 0), xn[s]).then_inc(xn_in_psum[s], 1)

            def project_pad(dst, w, act_t):
                for c in range(C):
                    for k in range(KC):
                        ins = pe.matmul(dst[:, c * P:(c + 1) * P], w[:, k, c * P:(c + 1) * P], act_t[:, k, :],
                                        start=(k == 0), stop=(k == KC - 1))
                return ins

            def q_and_k_layer1(s, it):
                pe.wait_ge(xn_t_ready[s], it + 1)
                project_pad(bank(s, 1), wq_pad, xn_t[s]).then_inc(q_in_psum[s], 1)
                pe.wait_ge(k_pad_ready[s], it + 1)
                for c in range(C):
                    ins = pe.transpose(bank(s, 2)[:, c * P:(c + 1) * P],
                                       k_pad[s][:, G * c:G * c + G, :].rearrange("p g w -> p (g w)"), ident[:, :])
                ins.then_inc(k_in_psum[s], 1)

            def head(t, c, g):
                return t[SLOT * g:SLOT * g + SLOT, c, :]

            def four(m):
                return m[:, :].unsqueeze(1).to_broadcast([P, C, P])

            def scores(s, u):
                pe.wait_ge(masks_ready[s], u + 1)
                pe.wait_ge(q_t_ready[s], u + 1)
                pe.wait_ge(k_t_ready[s], u + 1)
                for g in range(G):
                    pe.matmul(bank(s, g)[:, :].rearrange("p (c m) -> p c m", c=C), ident_b[:, :], four(neg_l[s]),
                              start=True, stop=False, skip_group_check=True)
                for c in range(C):
                    for g in range(G):
                        ins = pe.matmul(bank(s, g)[:, c * P:(c + 1) * P], head(q_t[s], c, g), head(k_t[s], c, g),
                                        start=False, stop=(c == C - 1), skip_group_check=True)
                ins.then_inc(scores_ready[s], 1)

            def turn_max(s, u):
                pe.wait_ge(max_ready[s], u + 1)
                for c in range(C):
                    ins = pe.transpose(bank(s, 0)[:, c * P:(c + 1) * P],
                                       max_pad[s][:, c, :, :].rearrange("p g w -> p (g w)"), ident[:, :])
                ins.then_inc(max_in_psum[s], 1)

            def scores_turned(s, u):
                for g in (1, 2, 3, 0):
                    if g == 0:
                        pe.wait_ge(q_aug_ready[s], u + 1)
                    pe.matmul(bank(s, g)[:, :].rearrange("p (c m) -> p c m", c=C), ident_b[:, :], four(neg_t[s]),
                              start=True, stop=False, skip_group_check=True)
                for c in range(C):
                    for g in range(G):
                        ins = pe.matmul(bank(s, g)[:, c * P:(c + 1) * P], head(k_t[s], c, g), head(q_aug[s], c, g),
                                        start=False, stop=(c == C - 1), skip_group_check=True)
                ins.then_inc(scores_t_ready[s], 1)

            def weigh_values(s, u, v, v_sem, n):
                pe.wait_ge(v_sem[s], n)
                for g in range(G):
                    pe.wait_ge(probs_ready[s], G * u + g + 1)
                    for c in range(C):
                        hh = G * c + g
                        ins = pe.matmul(bank(s, 0)[:, hh * (HD + 1):(hh + 1) * (HD + 1)], probs[s][:, g, c, :],
                                        v[s][:, hh, :], start=True, stop=True)
                ins.then_inc(pv_ready[s], 1)

            def turn_attn(s, u):
                pe.wait_ge(attn_ready[s], u + 1)
                turn(bank(s, 1), attn[s]).then_inc(attn_in_psum[s], 1)

            def mix_heads(s, u, w):
                pe.wait_ge(attn_t_ready[s], u + 1)
                for k in range(KC):
                    ins = pe.matmul(bank(s, 2)[:, 0:D], attn_t[s][:, k, :], w[:, k, :], start=(k == 0), stop=(k == KC - 1))
                ins.then_inc(mixed_ready[s], 1)

            def turn_score(s, it):
                pe.wait_ge(score_ready[s], it + 1)
                pe.transpose(bank(s, 0)[:, 0:P], score_wide[s][:, :], ident[:, :]).then_inc(score_in_psum[s], 1)

            def turn_h(s, it):
                pe.wait_ge(h_ready[s], it + 1)
                turn(bank(s, 3), h[s]).then_inc(h_in_psum[s], 1)

            def qkv_layer2(s, it):
                pe.wait_ge(h_t_ready[s], it + 1)
                project_pad(bank(s, 1), wq2_pad, h_t[s]).then_inc(q_in_psum[s], 1)
                project_pad(bank(s, 2), wk2_pad, h_t[s]).then_inc(k_in_psum[s], 1)
                for k in range(KC):
                    ins = pe.matmul(bank(s, 3)[:, 0:D], h_t[s][:, k, :], wv2[:, k, :], start=(k == 0), stop=(k == KC - 1))
                ins.then_inc(v_in_psum[s], 1)

            def turn_h2(s, it):
                pe.wait_ge(h2_ready[s], it + 1)
                turn(bank(s, 0), h2[s]).then_inc(h2_in_psum[s], 1)

            def ff_place(s, n, first, second):
                return (bank(s, first)[:, n * P:(n + 1) * P] if n < 4 else bank(s, second)[:, (n - 4) * P:(n - 3) * P])

            def ff_up(s, it):
                pe.wait_ge(h2_t_ready[s], it + 1)
                for w, first, second, done in ((w1_pad, 1, 2, ff_a_ready), (w2_pad, 3, 0, ff_b_ready)):
                    for n in range(FC):
                        for k in range(KC):
                            ins = pe.matmul(ff_place(s, n, first, second), w[:, k, n * P:(n + 1) * P], h2_t[s][:, k, :],
                                            start=(k == 0), stop=(k == KC - 1))
                    ins.then_inc(done[s], 1)

            def ff_down(s, it):
                pe.wait_ge(hidden_ready[s], it + 1)
                for n in range(FC):
                    ins = pe.matmul(bank(s, 1)[:, 0:D], hidden[s][:, n * P:(n + 1) * P], w3_pad[:, n, :],
                                    start=(n == 0), stop=(n == FC - 1))
                ins.then_inc(ff_ready[s], 1)

            def attention(it, layer):
                u = 2 * it + layer
                for s in range(NS):
                    if layer == 1:
                        pe.wait_ge(v2_ready[s], it + 1)
                    scores(s, u)
                for s in range(NS):
                    turn_max(s, u)
                    scores_turned(s, u)
                for s in range(NS):
                    if layer == 0:
                        weigh_values(s, u, v1, v1_ready, it + 1)
                    else:
                        weigh_values(s, u, v2, v2_ready, it + 1)
                for s in range(NS):
                    turn_attn(s, u)
                for s in range(NS):
                    mix_heads(s, u, wo_sb if layer == 0 else wout_sb)

            pe.wait_ge(weights_ready, 1)
            pe.wait_ge(consts_ready, 1 + NS)
            with pe.Fori(0, NB) as it:
                for s in range(NS):
                    turn_xn(s, it)
                for s in range(NS):
                    q_and_k_layer1(s, it)
                attention(it, 0)
                for s in range(NS):
                    turn_score(s, it)
                    turn_h(s, it)
                for s in range(NS):
                    qkv_layer2(s, it)
                attention(it, 1)
                for s in range(NS):
                    turn_h2(s, it)
                for s in range(NS):
                    ff_up(s, it)
                for s in range(NS):
                    ff_down(s, it)

        @block.vector
        def _(dve):
            dve.memset(w3_pad[:, FC - 1, :], 0.0).then_inc(dve_const, 1)
            dve.wait_ge(bucket_loaded, 16)
            for e in range(E):
                ins = dve.tensor_scalar(onehot[:, e, :], bucket_i[:, :], float(e), None, ALU.is_equal)
            ins.then_inc(route, 1)
            dve.wait_ge(route, 1)
            dve.tensor_copy(onehot_b[:, :, :], onehot[:, :, :]).then_inc(onehot_ready, 1)
            dve.wait_ge(consts_ready, 1)
            dve.wait_ge(counts_ready, 1)
            flat = "p e b -> p (e b)"
            dve.tensor_tensor_scan(totals_scan[:, :, :].rearrange(flat), scan_keep[:, :, :].rearrange(flat),
                                   banks[7][:, 0:P], 0.0, ALU.mult, ALU.add).then_inc(route, 1)
            dve.wait_ge(route, 2)
            dve.tensor_tensor(over[:, :, :], totals_scan[:, :, B - 1:B].to_broadcast([P, E, B]),
                              tile_marks[:, :].unsqueeze(1).to_broadcast([P, E, B]), ALU.is_gt).then_inc(route, 1)
            dve.tensor_tensor(rank[:, :, :].rearrange(flat), totals_scan[:, :, :].rearrange(flat), banks[7][:, 0:P],
                              ALU.subtract).then_inc(route, 1)
            dve.wait_ge(route, 4)
            dve.tensor_tensor(rank[:, :, :].rearrange(flat), rank[:, :, :].rearrange(flat), banks[6][:, 0:P],
                              ALU.add).then_inc(route, 1)
            dve.tensor_reduce(tiles_e[:, :], over[:, :, :], AX.X, ALU.add).then_inc(route, 1)
            dve.wait_ge(route, 6)
            dve.tensor_tensor_scan(tiles_end[:, :], ones_e[:, :], tiles_e[:, :], 0.0, ALU.mult, ALU.add).then_inc(route, 1)
            dve.wait_ge(route, 7)
            dve.tensor_tensor(tiles_base[:, :], tiles_end[:, :], tiles_e[:, :], ALU.subtract).then_inc(route, 1)
            dve.tensor_tensor(past[:, :, :], tiles_end[0:1, :].unsqueeze(1).to_broadcast([1, NTILE, E]),
                              tile_ids[0:1, :].unsqueeze(2).to_broadcast([1, NTILE, E]), ALU.is_le).then_inc(route, 1)
            dve.wait_ge(route, 9)
            dve.scalar_tensor_tensor(rank[:, :, :], tiles_base[:, :].unsqueeze(2).to_broadcast([P, E, B]), float(P),
                                     rank[:, :, :], ALU.mult, ALU.add).then_inc(route, 1)
            dve.tensor_reduce(expert_f[:, :], past[:, :, :], AX.X, ALU.add).then_inc(route, 1)
            dve.wait_ge(route, 11)
            dve.tensor_tensor(rank[:, :, :], rank[:, :, :], onehot[:, :, :], ALU.mult).then_inc(route, 1)
            dve.tensor_scalar(expert_i[:, :], expert_f[:, :], float(E - 1), None, ALU.min).then_inc(experts_ready, 1)
            dve.wait_ge(route, 12)
            dve.tensor_reduce(slot_f[:, :], rank[:, :, :].rearrange("p e b -> p b e"), AX.X, ALU.add).then_inc(route, 1)
            dve.wait_ge(route, 13)
            dve.tensor_copy(slot_u[:, :], slot_f[:, :]).then_inc(slots_ready, 1)

            for t in (wq_pad, wq2_pad, wk2_pad):
                dve.memset(t[:, :, :], 0.0)
            for t in (w1_pad, w2_pad):
                ins = dve.memset(t[:, :, DFF:DFFP], 0.0)
            ins.then_inc(dve_const, 1)
            dve.wait_ge(dve_const, 2)
            dve.wait_ge(weights_loaded, 16 * 8)
            dve.wait_ge(small_loaded, 16 * 8)

            def padded(t, k):
                return t[:, k, :].rearrange("p (h w) -> p h w", h=H)[:, :, 0:HD]

            def heads(t):
                return t.rearrange("p (h d) -> p h d", h=H)

            for k in range(KC):
                dve.tensor_copy(padded(wq_pad, k), heads(raw_q[:, k, :]))
                dve.tensor_scalar(padded(wq2_pad, k), heads(raw_qkv[:, k, 0:D]), g1_col[:, k:k + 1], None, ALU.mult)
                dve.tensor_scalar(padded(wk2_pad, k), heads(raw_qkv[:, k, D:2 * D]), g1_col[:, k:k + 1], None, ALU.mult)
                dve.tensor_scalar(wv2[:, k, :], raw_qkv[:, k, 2 * D:3 * D], g1_col[:, k:k + 1], None, ALU.mult)
                dve.tensor_scalar(w1_pad[:, k, 0:DFF], raw_ff[:, 0, k, :], g2_col[:, k:k + 1], None, ALU.mult)
                dve.tensor_scalar(w2_pad[:, k, 0:DFF], raw_ff[:, 1, k, :], g2_col[:, k:k + 1], None, ALU.mult)
            dve.wait_ge(rows_loaded, 32)
            dve.tensor_scalar(open_rows[:, :], pad_rows[:, :], -NEG, NEG, ALU.mult, ALU.add)
            dve.tensor_scalar(open_cols[:, :], pad_cols[:, :], -NEG, NEG, ALU.mult, ALU.add)
            dve.wait_ge(gates_ready, 1)
            dve.tensor_scalar(bias_row[:, :], bias_row[:, :], gates[:, 0:1], None, ALU.mult).then_inc(weights_ready, 1)
            dve.wait_ge(weights_ready, 1)

            dve.wait_ge(table_turned, 1)
            dve.tensor_copy(table_cols[:, :], banks[5][:, 0:NTILE]).then_inc(table_ready, 1)
            with dve.Fori(0, NTILE // UN) as i:
                for j in range(UN):
                    dve.wait_ge(kv_in_psum[j], i + 1)
                    dve.wait_ge(kv_stored[j], 16 * i)
                    dve.tensor_copy(tile_kv[j][:, :], banks[2 + j][:, :]).then_inc(kv_copied[j], 1)

            STEPS = 21

            class Chain:
                def __init__(self, s, it):
                    self.s, self.base, self.n = s, STEPS * it, 0

            chains = {}

            def step(s, ins):
                chains[s].n += 1
                ins.then_inc(dve_step[s], 1)

            def last_step(s):
                dve.wait_ge(dve_step[s], chains[s].base + chains[s].n)

            def moments(s, src):
                step(s, dve.bn_stats(stats[s][:, :], src))
                last_step(s)
                dve.memset(dve_held[:, :], 0.0)
                step(s, dve.bn_aggr(mean_var[s][:, :], stats[s][:, :]))
                last_step(s)
                step(s, dve.tensor_scalar(pow_in[s][:, 0:1], mean_var[s][:, 1:2], LN_EPS, None, ALU.add))
                last_step(s)
                dve.scalar_tensor_tensor(pow_in[s][:, 1:2], pow_in[s][:, 0:1], RMS_EPS, mean_var[s][:, 1:2],
                                         ALU.mult, ALU.add).then_inc(pow_asked[s], 1)

            def time_masks(s, it):
                b = NS * it + s
                t_row = time_rows[:, bass.ds(b * P, P)]
                t_col = time_cols[:, bass.ds(b, 1)]
                step(s, dve.scalar_tensor_tensor(neg_l[s][:, :], t_row, t_col, open_rows[:, bass.ds(b * P, P)],
                                                 ALU.is_le, ALU.mult))
                dve.tensor_scalar(neg_t[s][:, :], t_row, t_col, open_cols[:, bass.ds(b, 1)], ALU.is_ge, ALU.mult
                                  ).then_inc(masks_ready[s], 1)
                last_step(s)
                step(s, dve.tensor_reduce(any_open[s][:, :], neg_l[s][:, :], AX.X, ALU.max))

            def normalise_x(s, it):
                dve.wait_ge(pow_ready[s], 3 * it + 1)
                last_step(s)
                step(s, dve.scalar_tensor_tensor(q_rstd[s][:, :], any_open[s][:, :], 0.0, pow_out[s][:, 0:1],
                                                 ALU.is_equal, ALU.mult))
                last_step(s)
                dve.tensor_scalar(xn[s][:, :], x_sb[s][:, :], mean_var[s][:, 0:1], q_rstd[s][:, 0:1],
                                  ALU.subtract, ALU.mult).then_inc(xn_ready[s], 1)

            def maxima(s, u):
                dve.wait_ge(scores_ready[s], u + 1)
                for g in range(G):
                    ins = dve.tensor_reduce(max_pad[s][:, :, g, HD], bank(s, g)[:, :].rearrange("p (c m) -> p c m", c=C),
                                            AX.X, ALU.max)
                ins.then_inc(max_ready[s], 1)

            def join_max(s, u):
                dve.wait_ge(max_in_psum[s], u + 1)
                dve.tensor_tensor(q_aug[s][:, :, :], bank(s, 0)[:, :].rearrange("p (c m) -> p c m", c=C), q_t[s][:, :, :],
                                  ALU.add).then_inc(q_aug_ready[s], 1)

            def divide(s, u):
                dve.wait_ge(pv_ready[s], u + 1)
                o = bank(s, 0)[:, 0:H * (HD + 1)].rearrange("p (h d) -> p h d", h=H)
                step(s, dve.reciprocal(denom[s][:, :].unsqueeze(2), o[:, :, HD:HD + 1]))
                last_step(s)
                dve.tensor_tensor(attn[s][:, :].rearrange("p (h d) -> p h d", h=H), o[:, :, 0:HD],
                                  denom[s][:, :].unsqueeze(2).to_broadcast([P, H, HD]), ALU.mult).then_inc(attn_ready[s], 1)

            def residual1(s, it):
                dve.wait_ge(mixed_ready[s], 2 * it + 1)
                dve.wait_ge(x_bias_ready[s], it + 1)
                step(s, dve.scalar_tensor_tensor(x1[s][:, :], bank(s, 2)[:, 0:D], gates[:, 0:1], x_bias[s][:, :],
                                                 ALU.mult, ALU.add))
                last_step(s)

            def normalise_x1(s, it):
                dve.wait_ge(pow_ready[s], 3 * it + 2)
                step(s, dve.tensor_scalar(y[s][:, :], x1[s][:, :], mean_var[s][:, 0:1], pow_out[s][:, 0:1],
                                          ALU.subtract, ALU.mult))
                dve.tensor_scalar(h[s][:, :], x1[s][:, :], mean_var[s][:, 0:1], pow_out[s][:, 1:2],
                                  ALU.subtract, ALU.mult).then_inc(h_ready[s], 1)
                last_step(s)
                step(s, dve.tensor_tensor_reduce(junk[s][:, :], y[s][:, :], router_row[:, :], 1.0, 0.0, ALU.mult,
                                                 ALU.add, score[s][:, 0:1]))
                last_step(s)
                dve.tensor_copy(score_wide[s][:, :], score[s][:, 0:1].to_broadcast([P, P])).then_inc(score_ready[s], 1)

            def rank_masks(s, it):
                dve.wait_ge(score_in_psum[s], it + 1)
                row, col = bank(s, 0)[:, 0:P], score[s][:, 0:1]
                dve.scalar_tensor_tensor(mask_a[s][:, :], row, col, later_neg[:, :], ALU.is_le, ALU.mult)
                step(s, dve.tensor_scalar(mask_b[s][:, :], row, col, NEG, ALU.is_lt, ALU.mult))
                last_step(s)
                step(s, dve.tensor_tensor(neg_l[s][:, :], mask_a[s][:, :], mask_b[s][:, :], ALU.min))
                last_step(s)
                dve.scalar_tensor_tensor(mask_a[s][:, :], row, col, earlier_neg[:, :], ALU.is_ge, ALU.mult)
                step(s, dve.tensor_scalar(mask_b[s][:, :], row, col, NEG, ALU.is_gt, ALU.mult))
                last_step(s)
                dve.tensor_tensor(neg_t[s][:, :], mask_a[s][:, :], mask_b[s][:, :], ALU.min).then_inc(masks_ready[s], 1)

            def residual2(s, it):
                dve.wait_ge(mixed_ready[s], 2 * it + 2)
                step(s, dve.tensor_tensor(x2[s][:, :], bank(s, 2)[:, 0:D], y[s][:, :], ALU.add))
                last_step(s)
                step(s, dve.tensor_tensor_reduce(junk[s][:, :], x2[s][:, :], x2[s][:, :], 1.0 / D, 0.0, ALU.mult,
                                                 ALU.add, score[s][:, 0:1]))
                last_step(s)
                dve.tensor_scalar(pow_in[s][:, :], score[s][:, 0:1].to_broadcast([P, 2]), RMS_EPS, None, ALU.add
                                  ).then_inc(pow_asked[s], 1)

            def normalise_x2(s, it):
                dve.wait_ge(pow_ready[s], 3 * it + 3)
                dve.tensor_scalar(h2[s][:, :], x2[s][:, :], pow_out[s][:, 0:1], None, ALU.mult).then_inc(h2_ready[s], 1)

            def swiglu(s, it):
                dve.wait_ge(tanh_ready[s], it + 1)
                dve.scalar_tensor_tensor(silu_a[s][:, 0:512], tanh_a[s][:, 0:512], 1.0, bank(s, 1)[:, :], ALU.add, ALU.mult)
                step(s, dve.scalar_tensor_tensor(silu_a[s][:, 512:DFFP], tanh_a[s][:, 512:DFFP], 1.0,
                                                 bank(s, 2)[:, 0:DFFP - 512], ALU.add, ALU.mult))
                dve.wait_ge(ff_b_ready[s], it + 1)
                last_step(s)
                dve.scalar_tensor_tensor(hidden[s][:, 0:512], bank(s, 3)[:, :], 0.5, silu_a[s][:, 0:512], ALU.mult, ALU.mult)
                dve.scalar_tensor_tensor(hidden[s][:, 512:DFFP], bank(s, 0)[:, 0:DFFP - 512], 0.5, silu_a[s][:, 512:DFFP],
                                         ALU.mult, ALU.mult).then_inc(hidden_ready[s], 1)

            def residual3(s, it):
                dve.wait_ge(ff_ready[s], it + 1)
                step(s, dve.tensor_tensor(x3[s][:, :], bank(s, 1)[:, 0:D], x2[s][:, :], ALU.add))
                dve.wait_ge(out_stored[s], 16 * it)
                last_step(s)
                dve.scalar_tensor_tensor(y_out[s][:, :], x3[s][:, :], gates[:, 1:2], x1[s][:, :], ALU.mult, ALU.add
                                         ).then_inc(out_ready[s], 1)

            with dve.Fori(0, NB) as it:
                for s in range(NS):
                    chains[s] = Chain(s, it)
                    dve.wait_ge(x_loaded[s], 16 * it + 16)
                    moments(s, x_sb[s][:, :])
                    time_masks(s, it)
                for s in range(NS):
                    normalise_x(s, it)
                for s in range(NS):
                    maxima(s, 2 * it)
                for s in range(NS):
                    join_max(s, 2 * it)
                for s in range(NS):
                    divide(s, 2 * it)
                for s in range(NS):
                    residual1(s, it)
                    moments(s, x1[s][:, :])
                for s in range(NS):
                    normalise_x1(s, it)
                for s in range(NS):
                    rank_masks(s, it)
                for s in range(NS):
                    maxima(s, 2 * it + 1)
                for s in range(NS):
                    join_max(s, 2 * it + 1)
                for s in range(NS):
                    divide(s, 2 * it + 1)
                for s in range(NS):
                    residual2(s, it)
                for s in range(NS):
                    normalise_x2(s, it)
                for s in range(NS):
                    swiglu(s, it)
                for s in range(NS):
                    residual3(s, it)
                for s in range(NS):
                    assert chains[s].n == STEPS, chains[s].n


_ORDER = ["x", "ctx", "times", "times_t", "bucket_t", "pad", "pad_t", "g_x", "g_f", "wq", "wkv", "wo", "bo",
          "w_router", "wqkv_t", "wout_t", "g1", "g2", "w1t", "w2t", "w3t"]


def kernel(x, ctx_1024, fside_BxS2_0, itok_BxS2_0_7, mask_BxS2_bf0, g_xattn, g_ffn, L0_xattn_Wq, L0_xattn_Wk_b,
           L0_xattn_Wv_b, L0_xattn_Wo, L0_xattn_bo, L0_ffn_w_router, L0_ffn_W_qkv, L0_ffn_W_out, L0_ffn_g1,
           L0_ffn_g2, L0_ffn_W1, L0_ffn_W2, L0_ffn_W3):
    import concourse.bacc as bacc
    from concourse.bass_utils import run_bass_kernel_spmd

    lay = lambda a: np.ascontiguousarray(a)
    wkv = np.concatenate([np.asarray(L0_xattn_Wk_b), np.asarray(L0_xattn_Wv_b)], axis=-1)
    wkv = wkv.reshape(E, KC, P, 2 * D).transpose(2, 1, 0, 3).reshape(P, KC * E * 2 * D)
    pad = lay(mask_BxS2_bf0)
    data = {
        "x": lay(x), "ctx": lay(ctx_1024).reshape(B * P, D), "times": lay(fside_BxS2_0),
        "times_t": lay(np.asarray(fside_BxS2_0).T), "bucket_t": lay(np.asarray(itok_BxS2_0_7).T),
        "pad": pad, "pad_t": lay(pad.T), "g_x": lay(g_xattn), "g_f": lay(g_ffn), "wq": lay(L0_xattn_Wq),
        "wkv": lay(wkv), "wo": lay(L0_xattn_Wo), "bo": lay(L0_xattn_bo), "w_router": lay(L0_ffn_w_router),
        "wqkv_t": lay(np.asarray(L0_ffn_W_qkv).T), "wout_t": lay(np.asarray(L0_ffn_W_out).T),
        "g1": lay(np.asarray(L0_ffn_g1).reshape(KC, P).T), "g2": lay(np.asarray(L0_ffn_g2).reshape(KC, P).T), "w1t": lay(np.asarray(L0_ffn_W1).T),
        "w2t": lay(np.asarray(L0_ffn_W2).T), "w3t": lay(np.asarray(L0_ffn_W3).T),
    }
    nc = bacc.Bacc("TRN2", target_bir_lowering=False, num_devices=1)
    arrays, args = {}, []
    for name in _ORDER:
        arrays[f"in_{name}"] = data[name]
        args.append(nc.dram_tensor(f"in_{name}", data[name].shape, mybir.dt.from_np(data[name].dtype),
                                   kind="ExternalInput").ap())
    args.append(nc.dram_tensor("out_0", (B, P, D), F32, kind="ExternalOutput").ap())
    build(nc, *args)
    r = run_bass_kernel_spmd(nc, [arrays], core_ids=[0])
    return r.results[0]["out_0"]
```

```python
import numpy as np
import concourse.bass as bass
from concourse import mybir
from contextlib import ExitStack

F32 = mybir.dt.float32
BF16 = mybir.dt.bfloat16
I32 = mybir.dt.int32
U32 = mybir.dt.uint32
U8 = mybir.dt.uint8
ALU = mybir.AluOpType
ACT = mybir.ActivationFunctionType
AX = mybir.AxisListType

P = 128
B = 16
D = 256
KC = D // P
H = 16
HD = D // H
G = 4
C = H // G
SLOT = P // G
E = 8
NTILE = B + E
DFF = 682
FC = 6
DFFP = FC * P
NEG = -float(2 ** 100)
SCALE = 1.0 / float(HD) ** 0.5
LN_EPS = 1e-5
RMS_EPS = 1e-6
NS = 2
NB = B // NS
UN = 4


def at_least(eng, sem, n):
    if not (isinstance(n, int) and n == 0):
        eng.wait_ge(sem, n)


def turns(eng, n, body):
    body(0)
    with eng.Fori(1, n) as i:
        body(i)


def build(nc, x, ctx_in, times, times_t, bucket_t, pad, pad_t, g_x, g_f, wq, wkv, wo, bo,
          w_router, wqkv_t, wout_t, g1, g2, w1t, w2t, w3t, out):
    stack = ExitStack()
    with stack:
        def sb(name, shape, dt=F32):
            return stack.enter_context(nc.sbuf_tensor(name, shape, dt))

        def pair(name, shape, dt=F32):
            return [sb(f"{name}{s}", shape, dt) for s in range(NS)]

        def sem(name):
            return stack.enter_context(nc.semaphore(name))

        def sems(name, n=NS):
            return [sem(f"{name}{s}") for s in range(n)]

        token_of_slot = nc.dram_tensor("token_of_slot", [NTILE * P, 1], F32, kind="Internal").ap()
        kv_sorted = nc.dram_tensor("kv_sorted", [NTILE * P, 2 * D], F32, kind="Internal").ap()

        ident = sb("ident", [P, P])
        ident_b = sb("ident_b", [P, P], BF16)
        ones_b = sb("ones_b", [P, P], BF16)
        before_b = sb("before_b", [P, P], BF16)
        later_neg = sb("later_neg", [P, P])
        earlier_neg = sb("earlier_neg", [P, P])
        neg_half = sb("neg_half", [P, 2])
        pool_held = sb("pool_held", [1, 1])
        dve_held = sb("dve_held", [1, 1])
        minus_one_rows = sb("minus_one_rows", [P, 1])
        tile_marks = sb("tile_marks", [P, B])
        tile_ids = sb("tile_ids", [P, NTILE])
        token_ids_i = sb("token_ids_i", [P, B], I32)
        token_ids = sb("token_ids", [P, B])
        scan_keep = sb("scan_keep", [P, E, B])
        ones_e = sb("ones_e", [P, E])
        wkv_sb = sb("wkv_sb", [P, KC, E, 2 * D])
        raw_q = sb("raw_q", [P, KC, D])
        wq_pad = sb("wq_pad", [P, KC, H * SLOT])
        wo_pad = sb("wo_pad", [P, C, D])
        raw_qkv = sb("raw_qkv", [P, KC, 3 * D])
        wq2_pad = sb("wq2_pad", [P, KC, H * SLOT])
        wk2_pad = sb("wk2_pad", [P, KC, H * SLOT])
        wv2 = sb("wv2", [P, KC, D])
        wout_pad = sb("wout_pad", [P, C, D])
        raw_ff = sb("raw_ff", [P, 2, KC, DFF])
        w1_pad = sb("w1_pad", [P, KC, DFFP])
        w2_pad = sb("w2_pad", [P, KC, DFFP])
        w3_pad = sb("w3_pad", [P, FC, D])
        g1_col = sb("g1_col", [P, KC])
        g2_col = sb("g2_col", [P, KC])
        router_row = sb("router_row", [P, D])
        bias_row = sb("bias_row", [P, D])
        gates = sb("gates", [P, 2])
        gates_raw = sb("gates_raw", [P, 2])
        time_rows = sb("time_rows", [P, B * P])
        time_cols = sb("time_cols", [P, B])
        pad_rows = sb("pad_rows", [P, B * P], U8)
        pad_cols = sb("pad_cols", [P, B], U8)
        open_rows = sb("open_rows", [P, B * P], BF16)
        open_cols = sb("open_cols", [P, B])

        bucket_i = sb("bucket_i", [P, B], I32)
        onehot = sb("onehot", [P, E, B])
        onehot_b = sb("onehot_b", [P, E, B], BF16)
        totals_scan = sb("totals_scan", [P, E, B])
        rank = sb("rank", [P, E, B])
        over = sb("over", [P, E, B])
        tiles_e = sb("tiles_e", [P, E])
        tiles_end = sb("tiles_end", [P, E])
        tiles_base = sb("tiles_base", [P, E])
        slot_f = sb("slot_f", [P, B])
        slot_u = sb("slot_u", [P, B], U32)
        past = sb("past", [1, NTILE, E])
        expert_f = sb("expert_f", [1, NTILE])
        expert_i = sb("expert_i", [1, NTILE], I32)
        table_zero = sb("table_zero", [NTILE, P])
        table_rows = sb("table_rows", [NTILE, P])
        table_cols = sb("table_cols", [P, NTILE], U32)
        tile_index = sb("tile_index", [P, UN], U32)

        x_sb = pair("x_sb", [P, D])
        kv_index = pair("kv_index", [P, 1], U32)
        kv_raw = pair("kv_raw", [P, 2 * D])
        k_pad = pair("k_pad", [P, H, SLOT])
        v1 = pair("v1", [P, H, SLOT])
        v2 = pair("v2", [P, H, SLOT])
        x_bias = pair("x_bias", [P, D])
        stats = pair("stats", [P, 6])
        mean_var = pair("mean_var", [P, 2])
        pow_in = pair("pow_in", [P, 2])
        pow_out = pair("pow_out", [P, 2])
        any_open = pair("any_open", [P, 1])
        q_rstd = pair("q_rstd", [P, 1])
        neg_l = pair("neg_l", [P, P], BF16)
        neg_t = pair("neg_t", [P, P], BF16)
        mask_a = pair("mask_a", [P, P])
        mask_b = pair("mask_b", [P, P])
        xn = pair("xn", [P, D])
        xn_t = pair("xn_t", [P, KC, P])
        q_t = pair("q_t", [P, C, P])
        k_t = pair("k_t", [P, C, P])
        q_aug = pair("q_aug", [P, C, P])
        max_pad = pair("max_pad", [P, C, G, SLOT])
        probs = pair("probs", [P, G, C, P])
        denom = pair("denom", [P, H])
        mixed_blocks = pair("mixed_blocks", [P, H, SLOT])
        attn_blocks = pair("attn_blocks", [P, H, SLOT])
        attn_t = pair("attn_t", [P, C, P])
        x1 = pair("x1", [P, D])
        y = pair("y", [P, D])
        junk = pair("junk", [P, D])
        score = pair("score", [P, 1])
        score_wide = pair("score_wide", [P, P])
        h = pair("h", [P, D])
        h_t = pair("h_t", [P, KC, P])
        x2 = pair("x2", [P, D])
        h2 = pair("h2", [P, D])
        h2_t = pair("h2_t", [P, KC, P])
        probs_flat = [t[:, :, :, :].rearrange("p g c m -> p (g c m)") for t in probs]
        tanh_a = [t[:, 0:DFFP] for t in probs_flat]
        silu_a = tanh_a
        hidden = [t[:, DFFP:2 * DFFP] for t in probs_flat]
        tile_kv = [probs_flat[0][:, j * 2 * D:(j + 1) * 2 * D] for j in range(UN)]
        tile_ctx = [probs_flat[1][:, j * D:(j + 1) * D] for j in range(UN)]
        tile_ctx_t = [probs_flat[1][:, (UN + j) * D:(UN + j + 1) * D].rearrange("p (k m) -> p k m", k=KC)
                      for j in range(2)]
        x3 = pair("x3", [P, D])
        y_out = pair("y_out", [P, D])

        banks = [stack.enter_context(nc.psum_tensor(f"bank{i}", [P, 512], F32)) for i in range(8)]

        def bank(s, g):
            return banks[4 * s + g]

        bucket_loaded = sem("bucket_loaded")
        small_loaded = sem("small_loaded")
        rows_loaded = sem("rows_loaded")
        weights_loaded = sem("weights_loaded")
        wkv_loaded = sem("wkv_loaded")
        pool_const = sem("pool_const")
        pool_step = sem("pool_step")
        pool_carried = sem("pool_carried")
        consts_ready = sem("consts_ready")
        dve_const = sem("dve_const")
        weights_ready = sem("weights_ready")
        route = sem("route")
        onehot_ready = sem("onehot_ready")
        counts_ready = sem("counts_ready")
        slots_ready = sem("slots_ready")
        experts_ready = sem("experts_ready")
        gates_ready = sem("gates_ready")
        table_zeroed = sem("table_zeroed")
        table_filled = sem("table_filled")
        table_loaded = sem("table_loaded")
        table_turned = sem("table_turned")
        table_ready = sem("table_ready")
        index_ready = sem("index_ready")
        ctx_gathered = sems("ctx_gathered", UN)
        ctx_turned = sems("ctx_turned", UN)
        ctx_t_ready = sems("ctx_t_ready", UN)
        kv_in_psum = sems("kv_in_psum", UN)
        kv_copied = sems("kv_copied", UN)
        kv_stored = sems("kv_stored", UN)

        x_loaded = sems("x_loaded")
        kv_index_ready = sems("kv_index_ready")
        kv_gathered = sems("kv_gathered")
        k_pad_ready = sems("k_pad_ready")
        v1_ready = sems("v1_ready")
        v2_ready = sems("v2_ready")
        x_bias_ready = sems("x_bias_ready")
        dve_step = sems("dve_step")
        pow_asked = sems("pow_asked")
        pow_ready = sems("pow_ready")
        masks_ready = sems("masks_ready")
        xn_ready = sems("xn_ready")
        xn_in_psum = sems("xn_in_psum")
        xn_t_ready = sems("xn_t_ready")
        q_in_psum = sems("q_in_psum")
        k_in_psum = sems("k_in_psum")
        v_in_psum = sems("v_in_psum")
        q_t_ready = sems("q_t_ready")
        k_t_ready = sems("k_t_ready")
        scores_ready = sems("scores_ready")
        max_ready = sems("max_ready")
        max_in_psum = sems("max_in_psum")
        q_aug_ready = sems("q_aug_ready")
        scores_t_ready = sems("scores_t_ready")
        probs_ready = sems("probs_ready")
        pv_ready = sems("pv_ready")
        attn_t_ready = sems("attn_t_ready")
        x1_ready = sems("x1_ready")
        mixed_ready = sems("mixed_ready")
        score_ready = sems("score_ready")
        score_in_psum = sems("score_in_psum")
        h_ready = sems("h_ready")
        h_in_psum = sems("h_in_psum")
        h_t_ready = sems("h_t_ready")
        h2_ready = sems("h2_ready")
        h2_in_psum = sems("h2_in_psum")
        h2_t_ready = sems("h2_t_ready")
        ff_a_ready = sems("ff_a_ready")
        ff_b_ready = sems("ff_b_ready")
        tanh_ready = sems("tanh_ready")
        hidden_ready = sems("hidden_ready")
        ff_ready = sems("ff_ready")
        out_ready = sems("out_ready")
        out_stored = sems("out_stored")

        block = stack.enter_context(nc.Block())

        @block.sync
        def _(sp):
            sp.dma_start(bucket_i[:, :], bucket_t).then_inc(bucket_loaded, 16)
            sp.dma_start(wkv_sb[:, :, :, :].rearrange("p a e n -> p (a e n)"), wkv).then_inc(wkv_loaded, 16)
            sp.wait_ge(table_filled, 16 * B)
            sp.dma_start(table_rows[:, :], token_of_slot.rearrange("(t m) o -> t (m o)", m=P)).then_inc(table_loaded, 16)

            def load_x(s, it):
                sp.dma_start(x_sb[s][:, :], x[bass.ds(NS * it + s, 1), :, :].rearrange("a p d -> (a p) d")
                             ).then_inc(x_loaded[s], 16)

            for s in range(NS):
                load_x(s, 0)
            def store_tiles(i):
                for j in range(UN):
                    sp.wait_ge(kv_copied[j], i + 1)
                    sp.dma_start(kv_sorted[bass.ds((UN * i + j) * P, P), :], tile_kv[j][:, :]).then_inc(kv_stored[j], 16)

            turns(sp, NTILE // UN, store_tiles)

            def half(it, s, has_x, has_z, more):
                if has_z:
                    sp.wait_ge(out_ready[s], it)
                    sp.dma_start(out[bass.ds(NS * (it - 1) + s, 1), :, :].rearrange("a p d -> (a p) d"), y_out[s][:, :]
                                 ).then_inc(out_stored[s], 16)
                if has_x and more:
                    sp.wait_ge(x_bias_ready[s], it + 1)
                    sp.wait_ge(xn_ready[s], it + 1)
                    load_x(s, it + 1)

            def rows(it, first=False, last=False, more=True):
                for s in range(NS):
                    half(it, s, not last, not first, more)

            rows(0, first=True)
            with sp.Fori(1, NB - 1) as it:
                rows(it)
            rows(NB - 1, more=False)
            rows(NB, last=True)
            for s in range(NS):
                sp.wait_ge(out_stored[s], 16 * NB)
            for j in range(UN):
                sp.wait_ge(kv_stored[j], 16 * (NTILE // UN))

        @block.gpsimd
        def _(pool):
            pool.memset(table_zero[:, :], 0.0).then_inc(pool_step, 1)
            pool.memset(ident[:, :], 0.0).then_inc(pool_const, 1)
            pool.memset(before_b[:, :], 1.0).then_inc(pool_const, 1)
            pool.memset(later_neg[:, :], NEG).then_inc(pool_const, 1)
            pool.memset(earlier_neg[:, :], NEG).then_inc(pool_const, 1)
            pool.memset(minus_one_rows[:, :], 0.0).then_inc(pool_const, 1)
            pool.memset(scan_keep[:, :, :], 1.0).then_inc(pool_const, 1)
            pool.iota(token_ids_i[:, :], pattern=[[P, B]], base=0, channel_multiplier=1).then_inc(pool_const, 1)
            pool.memset(ones_b[:, :], 1.0)
            pool.memset(ones_e[:, :], 1.0)
            pool.memset(neg_half[:, :], -0.5)
            pool.wait_ge(pool_step, 1)
            pool.dma_start(token_of_slot.rearrange("(t m) o -> t (m o)", m=P), table_zero[:, :]).then_inc(table_zeroed, 16)
            pool.wait_ge(pool_const, 7)
            pool.affine_select(out=ident[:, :], in_=ident[:, :], compare_op=ALU.not_equal, fill=1.0,
                               base=0, pattern=[[-1, P]], channel_multiplier=1).then_inc(pool_const, 1)
            pool.affine_select(out=before_b[:, :], in_=before_b[:, :], compare_op=ALU.is_gt, fill=0.0,
                               base=0, pattern=[[1, P]], channel_multiplier=-1)
            pool.affine_select(out=later_neg[:, :], in_=later_neg[:, :], compare_op=ALU.is_gt, fill=0.0,
                               base=0, pattern=[[1, P]], channel_multiplier=-1)
            pool.affine_select(out=earlier_neg[:, :], in_=earlier_neg[:, :], compare_op=ALU.is_gt, fill=0.0,
                               base=0, pattern=[[-1, P]], channel_multiplier=1)
            pool.affine_select(out=scan_keep[:, :, :], in_=scan_keep[:, :, :], compare_op=ALU.not_equal, fill=0.0,
                               base=0, pattern=[[0, E], [1, B]], channel_multiplier=0)
            for g in range(G):
                ins = pool.affine_select(out=minus_one_rows[:, :], in_=minus_one_rows[:, :], compare_op=ALU.not_equal,
                                         fill=-1.0, base=-(SLOT * g + HD), pattern=[[0, 1]], channel_multiplier=1)
                ins.then_inc(pool_const, 1)
                pool.wait_ge(pool_const, 9 + g)
            pool.tensor_copy(token_ids[:, :], token_ids_i[:, :])
            pool.iota(tile_marks[:, :], pattern=[[P, B]], base=0, channel_multiplier=0,
                      allow_small_or_imprecise_dtypes=True)
            pool.iota(tile_ids[:, :], pattern=[[1, NTILE]], base=0, channel_multiplier=0,
                      allow_small_or_imprecise_dtypes=True)
            pool.tensor_copy(ident_b[:, :], ident[:, :]).then_inc(consts_ready, 1)
            pool.wait_ge(consts_ready, 1)
            pool.wait_ge(table_zeroed, 16)
            pool.wait_ge(slots_ready, 1)
            for b in range(B):
                pool.indirect_dma_start(out=token_of_slot, out_offset=bass.IndirectOffsetOnAxis(ap=slot_u[:, b:b + 1], axis=0),
                                        in_=token_ids[:, b:b + 1], in_offset=None).then_inc(table_filled, 16)
            for s in range(NS):
                pool.memset(k_pad[s][:, :, :], 0.0)
                pool.memset(v1[s][:, :, :], 0.0)
                pool.memset(v2[s][:, :, :], 0.0)
                pool.memset(attn_blocks[s][:, :, :], 0.0)
                pool.memset(max_pad[s][:, :, :, :], 0.0).then_inc(consts_ready, 1)
            pool.wait_ge(consts_ready, 1 + NS)
            for s in range(NS):
                pool.memset(v1[s][:, :, HD:HD + 1], 1.0)
                pool.memset(v2[s][:, :, HD:HD + 1], 1.0).then_inc(consts_ready, 1)
            pool.wait_ge(consts_ready, 1 + 2 * NS)
            pool.wait_ge(table_ready, 1)
            def hold():
                pool.wait_ge(table_ready, 1)

            def carry(n):
                at_least(pool, pool_carried, n)
                pool.tensor_tensor(pool_held[:, :], neg_half[0:1, 0:1], neg_half[0:1, 0:1], ALU.add).then_inc(pool_carried, 1)

            def gather_tiles(i):
                hold()
                for j in range(UN):
                    at_least(pool, ctx_gathered[j], 16 * i)
                pool.tensor_copy(tile_index[:, :], table_cols[:, bass.ds(UN * i, UN)]).then_inc(index_ready, 1)
                for j in range(UN):
                    pool.wait_ge(index_ready, i + 1)
                    at_least(pool, ctx_turned[j], i)
                    carry(UN * i + j)
                    pool.indirect_dma_start(out=tile_ctx[j][:, :], out_offset=None, in_=ctx_in,
                                            in_offset=bass.IndirectOffsetOnAxis(ap=tile_index[:, j:j + 1], axis=0)
                                            ).then_inc(ctx_gathered[j], 16)

            turns(pool, NTILE // UN, gather_tiles)

            def gather_kv(s, it):
                pool.tensor_copy(kv_index[s][:, :], slot_u[:, bass.ds(NS * it + s, 1)]).then_inc(kv_index_ready[s], 1)
                pool.wait_ge(kv_index_ready[s], it + 1)
                carry(NTILE + NS * it + s)
                pool.indirect_dma_start(out=kv_raw[s][:, :], out_offset=None, in_=kv_sorted,
                                        in_offset=bass.IndirectOffsetOnAxis(ap=kv_index[s][:, 0:1], axis=0)
                                        ).then_inc(kv_gathered[s], 16)

            def spread_kv(s, it):
                pool.tensor_copy(k_pad[s][:, :, 0:HD], kv_raw[s][:, 0:D].rearrange("p (h d) -> p h d", h=H)
                                 ).then_inc(k_pad_ready[s], 1)
                pool.tensor_copy(v1[s][:, :, 0:HD], kv_raw[s][:, D:2 * D].rearrange("p (h d) -> p h d", h=H)
                                 ).then_inc(v1_ready[s], 1)

            def add_bias(s, it):
                pool.wait_ge(x_loaded[s], 16 * it + 16)
                at_least(pool, x1_ready[s], it)
                pool.tensor_tensor(x_bias[s][:, :], x_sb[s][:, :], bias_row[:, :], ALU.add).then_inc(x_bias_ready[s], 1)

            def power(s, it, k):
                if k == 0:
                    at_least(pool, h2_ready[s], it)
                pool.wait_ge(pow_asked[s], 3 * it + k + 1)
                if k == 0:
                    pool.wait_ge(kv_gathered[s], 16 * it + 16)
                    at_least(pool, k_in_psum[s], 2 * it)
                    at_least(pool, pv_ready[s], 2 * it)
                pool.tensor_tensor(pow_out[s][:, :], pow_in[s][:, :], neg_half[:, :], ALU.pow).then_inc(pow_ready[s], 1)

            for j in range(UN):
                pool.wait_ge(kv_stored[j], 16 * (NTILE // UN))
            for s in range(NS):
                gather_kv(s, 0)
            pool.wait_ge(weights_ready, 1)

            def half(it, s, has_x, y_it, more):
                if has_x:
                    power(s, it, 0)
                    spread_kv(s, it)
                    add_bias(s, it)
                    if more:
                        hold()
                        pool.wait_ge(v1_ready[s], it + 1)
                        gather_kv(s, it + 1)
                if y_it is not None:
                    power(1 - s, y_it, 2)
                if has_x:
                    power(s, it, 1)

            def rows(it, first=False, last=False, more=True):
                half(it, 0, not last, None if first else it - 1, more)
                if not last:
                    half(it, 1, True, it, more)

            rows(0, first=True)
            with pool.Fori(1, NB - 1) as it:
                rows(it)
            rows(NB - 1, more=False)
            rows(NB, last=True)

        @block.scalar
        def _(act):
            act.dma_start(gates_raw[:, 0:1], g_x.rearrange("(a n) -> a n", a=1).to_broadcast([P, 1])).then_inc(small_loaded, 16)
            act.dma_start(gates_raw[:, 1:2], g_f.rearrange("(a n) -> a n", a=1).to_broadcast([P, 1])).then_inc(small_loaded, 16)
            act.dma_start(g1_col[:, :], g1).then_inc(small_loaded, 16)
            act.dma_start(g2_col[:, :], g2).then_inc(small_loaded, 16)
            act.dma_start(time_cols[:, :], times_t).then_inc(small_loaded, 16)
            act.dma_start(pad_cols[:, :], pad_t).then_inc(small_loaded, 16)
            act.dma_start(router_row[:, :], w_router.rearrange("(a n) -> a n", a=1).to_broadcast([P, D])).then_inc(small_loaded, 16)
            act.dma_start(bias_row[:, :], bo.rearrange("(a n) -> a n", a=1).to_broadcast([P, D])).then_inc(small_loaded, 16)
            act.dma_start(time_rows[:, :], times.rearrange("(a b) t -> a (b t)", a=1).to_broadcast([P, B * P])).then_inc(rows_loaded, 16)
            act.dma_start(pad_rows[:, :], pad.rearrange("(a b) t -> a (b t)", a=1).to_broadcast([P, B * P])).then_inc(rows_loaded, 16)
            act.dma_start(raw_q[:, :, :], wq.rearrange("(k p) n -> p k n", p=P)).then_inc(weights_loaded, 16)
            act.dma_start(raw_qkv[:, :, :], wqkv_t.rearrange("(k p) n -> p k n", p=P)).then_inc(weights_loaded, 16)
            act.dma_start(raw_ff[:, 0, :, :], w1t.rearrange("(k p) n -> p k n", p=P)).then_inc(weights_loaded, 16)
            act.dma_start(raw_ff[:, 1, :, :], w2t.rearrange("(k p) n -> p k n", p=P)).then_inc(weights_loaded, 16)
            act.dma_start(w3_pad[:, 0:FC - 1, :], w3t[0:(FC - 1) * P, :].rearrange("(k p) n -> p k n", p=P)).then_inc(weights_loaded, 16)
            act.wait_ge(dve_const, 1)
            for g in range(G):
                for dst, src in ((wo_pad, wo), (wout_pad, wout_t)):
                    act.dma_start(dst[SLOT * g:SLOT * g + HD, :, :],
                                  src.rearrange("(c g j) n -> g j c n", c=C, g=G)[g]).then_inc(weights_loaded, 16)
            act.dma_start(w3_pad[0:DFF - (FC - 1) * P, FC - 1, :], w3t[(FC - 1) * P:DFF, :]).then_inc(weights_loaded, 16)
            act.wait_ge(small_loaded, 16 * 8)
            act.activation(gates[:, :], gates_raw[:, :], ACT.Tanh).then_inc(gates_ready, 1)

            def copy_tiles(i):
                for j in range(UN):
                    act.wait_ge(ctx_turned[j], i + 1)
                    act.activation(tile_ctx_t[j % 2][:, :, :], banks[j % 2][:, 0:D].rearrange("p (k m) -> p k m", k=KC),
                                   ACT.Copy).then_inc(ctx_t_ready[j], 1)

            turns(act, NTILE // UN, copy_tiles)

            def three(t):
                return t.rearrange("p (k m) -> p k m", k=KC)

            def copy_xn(s, it):
                act.wait_ge(xn_in_psum[s], it + 1)
                act.activation(xn_t[s][:, :, :], three(bank(s, 0)[:, 0:D]), ACT.Copy).then_inc(xn_t_ready[s], 1)

            def copy_qk(s, u):
                act.wait_ge(q_in_psum[s], u + 1)
                act.activation(q_t[s][:, :, :], bank(s, 1)[:, :].rearrange("p (c m) -> p c m", c=C),
                               ACT.Copy).then_inc(q_t_ready[s], 1)
                act.wait_ge(k_in_psum[s], u + 1)
                act.activation(k_t[s][:, :, :], bank(s, 2)[:, :].rearrange("p (c m) -> p c m", c=C),
                               ACT.Identity, bias=minus_one_rows[:, 0:1]).then_inc(k_t_ready[s], 1)

            def copy_v(s, it):
                act.wait_ge(v_in_psum[s], it + 1)
                act.activation(v2[s][:, :, 0:HD], bank(s, 3)[:, 0:D].rearrange("p (h d) -> p h d", h=H),
                               ACT.Copy).then_inc(v2_ready[s], 1)

            def exponentials(s, u):
                act.wait_ge(scores_t_ready[s], u + 1)
                for g in range(G):
                    act.activation(probs[s][:, g, :, :], bank(s, g)[:, :].rearrange("p (c m) -> p c m", c=C),
                                   ACT.Exp, scale=SCALE).then_inc(probs_ready[s], 1)

            def copy_h(s, it):
                act.wait_ge(h_in_psum[s], it + 1)
                act.activation(h_t[s][:, :, :], three(bank(s, 3)[:, 0:D]), ACT.Copy).then_inc(h_t_ready[s], 1)

            def copy_h2(s, it):
                act.wait_ge(h2_in_psum[s], it + 1)
                act.activation(h2_t[s][:, :, :], three(bank(s, 0)[:, 0:D]), ACT.Copy).then_inc(h2_t_ready[s], 1)

            def tanh_half(s, it):
                act.wait_ge(ff_a_ready[s], it + 1)
                act.activation(tanh_a[s][:, 0:512], bank(s, 1)[:, :], ACT.Tanh, scale=0.5)
                act.activation(tanh_a[s][:, 512:DFFP], bank(s, 2)[:, 0:DFFP - 512], ACT.Tanh, scale=0.5
                               ).then_inc(tanh_ready[s], 1)

            def half(it, s, has_x, y_it):
                t = 1 - s
                if y_it is not None:
                    copy_h(t, y_it)
                    copy_qk(t, 2 * y_it + 1)
                    copy_v(t, y_it)
                if has_x:
                    copy_xn(s, it)
                    copy_qk(s, 2 * it)
                if y_it is not None:
                    exponentials(t, 2 * y_it + 1)
                if has_x:
                    exponentials(s, 2 * it)
                if y_it is not None:
                    copy_h2(t, y_it)
                    tanh_half(t, y_it)

            def rows(it, first=False, last=False):
                half(it, 0, not last, None if first else it - 1)
                if not last:
                    half(it, 1, True, it)

            rows(0, first=True)
            with act.Fori(1, NB) as it:
                rows(it)
            rows(NB, last=True)

        @block.tensor
        def _(pe):
            pe.wait_ge(consts_ready, 1)
            pe.wait_ge(onehot_ready, 1)
            pe.matmul(banks[6][:, 0:P], before_b[:, :], onehot_b[:, :, :], start=True, stop=True)
            pe.matmul(banks[7][:, 0:P], ones_b[:, :], onehot_b[:, :, :], start=True, stop=True).then_inc(counts_ready, 1)
            pe.wait_ge(table_loaded, 16)
            pe.transpose(banks[5][:, 0:NTILE], table_rows[:, :], ident[0:NTILE, 0:NTILE]).then_inc(table_turned, 1)

            def turn(dst, src):
                for k in range(KC):
                    ins = pe.transpose(dst[:, k * P:(k + 1) * P], src[:, k * P:(k + 1) * P], ident[:, :])
                return ins

            def turn_tile(j, i):
                pe.wait_ge(ctx_gathered[j], 16 * i + 16)
                turn(banks[j % 2], tile_ctx[j]).then_inc(ctx_turned[j], 1)

            def project_tile(j, i):
                expert = nc.tensor.value_load(expert_i[0:1, bass.ds(UN * i + j, 1)], min_val=0, max_val=E - 1)
                pe.wait_ge(ctx_t_ready[j], i + 1)
                at_least(pe, kv_copied[j], i)
                for k in range(KC):
                    ins = pe.matmul(banks[2 + j][:, :], tile_ctx_t[j % 2][:, k, :],
                                    wkv_sb[:, k, bass.ds(expert, 1), :].rearrange("p a n -> p (a n)"),
                                    start=(k == 0), stop=(k == KC - 1))
                ins.then_inc(kv_in_psum[j], 1)

            pe.wait_ge(wkv_loaded, 16)
            pe.wait_ge(experts_ready, 1)
            pe.wait_ge(table_ready, 1)
            def tiles(i):
                turn_tile(0, i)
                for j in range(UN):
                    if j + 1 < UN:
                        if j + 1 >= 2:
                            pe.wait_ge(ctx_t_ready[j - 1], i + 1)
                        turn_tile(j + 1, i)
                    project_tile(j, i)

            turns(pe, NTILE // UN, tiles)

            def turn_xn(s, it):
                pe.wait_ge(xn_ready[s], it + 1)
                turn(bank(s, 0), xn[s]).then_inc(xn_in_psum[s], 1)

            def project_pad(dst, w, act_t):
                for c in range(C):
                    for k in range(KC):
                        ins = pe.matmul(dst[:, c * P:(c + 1) * P], w[:, k, c * P:(c + 1) * P], act_t[:, k, :],
                                        start=(k == 0), stop=(k == KC - 1))
                return ins

            def q_and_k_layer1(s, it):
                pe.wait_ge(k_pad_ready[s], it + 1)
                for c in range(C):
                    ins = pe.transpose(bank(s, 2)[:, c * P:(c + 1) * P],
                                       k_pad[s][:, G * c:G * c + G, :].rearrange("p g w -> p (g w)"), ident[:, :])
                ins.then_inc(k_in_psum[s], 1)
                pe.wait_ge(xn_t_ready[s], it + 1)
                project_pad(bank(s, 1), wq_pad, xn_t[s]).then_inc(q_in_psum[s], 1)

            def head(t, c, g):
                return t[SLOT * g:SLOT * g + SLOT, c, :]

            def four(m):
                return m[:, :].unsqueeze(1).to_broadcast([P, C, P])

            def scores(s, u):
                pe.wait_ge(masks_ready[s], u + 1)
                pe.wait_ge(q_t_ready[s], u + 1)
                pe.wait_ge(k_t_ready[s], u + 1)
                for g in range(G):
                    pe.matmul(bank(s, g)[:, :].rearrange("p (c m) -> p c m", c=C), ident_b[:, :], four(neg_l[s]),
                              start=True, stop=False, skip_group_check=True)
                for c in range(C):
                    for g in range(G):
                        ins = pe.matmul(bank(s, g)[:, c * P:(c + 1) * P], head(q_t[s], c, g), head(k_t[s], c, g),
                                        start=False, stop=(c == C - 1), skip_group_check=True)
                ins.then_inc(scores_ready[s], 1)

            def turn_max(s, u):
                pe.wait_ge(max_ready[s], u + 1)
                for c in range(C):
                    ins = pe.transpose(bank(s, 0)[:, c * P:(c + 1) * P],
                                       max_pad[s][:, c, :, :].rearrange("p g w -> p (g w)"), ident[:, :])
                ins.then_inc(max_in_psum[s], 1)

            def scores_turned(s, u):
                for g in (1, 2, 3, 0):
                    if g == 0:
                        pe.wait_ge(q_aug_ready[s], u + 1)
                    pe.matmul(bank(s, g)[:, :].rearrange("p (c m) -> p c m", c=C), ident_b[:, :], four(neg_t[s]),
                              start=True, stop=False, skip_group_check=True)
                for c in range(C):
                    for g in range(G):
                        ins = pe.matmul(bank(s, g)[:, c * P:(c + 1) * P], head(k_t[s], c, g), head(q_aug[s], c, g),
                                        start=False, stop=(c == C - 1), skip_group_check=True)
                ins.then_inc(scores_t_ready[s], 1)

            def weigh_values(s, u, v):
                for g in range(G):
                    pe.wait_ge(probs_ready[s], G * u + g + 1)
                    for c in range(C):
                        ins = pe.matmul(bank(s, 0)[SLOT * g:SLOT * g + SLOT, c * P:(c + 1) * P], v[s][:, G * c + g, :],
                                        probs[s][:, g, c, :], start=True, stop=True)
                ins.then_inc(pv_ready[s], 1)

            def mix_heads(s, u, w):
                pe.wait_ge(attn_t_ready[s], u + 1)
                for c in range(C):
                    ins = pe.matmul(bank(s, 2)[:, 0:D], attn_t[s][:, c, :], w[:, c, :], start=(c == 0), stop=(c == C - 1))
                ins.then_inc(mixed_ready[s], 1)

            def turn_score(s, it):
                pe.wait_ge(score_ready[s], it + 1)
                pe.transpose(bank(s, 0)[:, 0:P], score_wide[s][:, :], ident[:, :]).then_inc(score_in_psum[s], 1)

            def turn_h(s, it):
                pe.wait_ge(h_ready[s], it + 1)
                turn(bank(s, 3), h[s]).then_inc(h_in_psum[s], 1)

            def qkv_layer2(s, it):
                pe.wait_ge(h_t_ready[s], it + 1)
                project_pad(bank(s, 1), wq2_pad, h_t[s]).then_inc(q_in_psum[s], 1)
                project_pad(bank(s, 2), wk2_pad, h_t[s]).then_inc(k_in_psum[s], 1)
                for k in range(KC):
                    ins = pe.matmul(bank(s, 3)[:, 0:D], h_t[s][:, k, :], wv2[:, k, :], start=(k == 0), stop=(k == KC - 1))
                ins.then_inc(v_in_psum[s], 1)

            def turn_h2(s, it):
                pe.wait_ge(h2_ready[s], it + 1)
                turn(bank(s, 0), h2[s]).then_inc(h2_in_psum[s], 1)

            def ff_place(s, n, first, second):
                return (bank(s, first)[:, n * P:(n + 1) * P] if n < 4 else bank(s, second)[:, (n - 4) * P:(n - 3) * P])

            def ff_up(s, it):
                pe.wait_ge(h2_t_ready[s], it + 1)
                for w, first, second, done in ((w1_pad, 1, 2, ff_a_ready), (w2_pad, 3, 0, ff_b_ready)):
                    for n in range(FC):
                        for k in range(KC):
                            ins = pe.matmul(ff_place(s, n, first, second), w[:, k, n * P:(n + 1) * P], h2_t[s][:, k, :],
                                            start=(k == 0), stop=(k == KC - 1))
                    ins.then_inc(done[s], 1)

            def ff_down(s, it):
                pe.wait_ge(hidden_ready[s], it + 1)
                for n in range(FC):
                    ins = pe.matmul(bank(s, 3)[:, 0:D], hidden[s][:, n * P:(n + 1) * P], w3_pad[:, n, :],
                                    start=(n == 0), stop=(n == FC - 1))
                ins.then_inc(ff_ready[s], 1)

            pe.wait_ge(weights_ready, 1)
            pe.wait_ge(consts_ready, 1 + 2 * NS)

            def half(it, s, has_x, y_it, has_z):
                t = 1 - s
                has_y = y_it is not None
                if has_y:
                    turn_h(t, y_it)
                    turn_score(t, y_it)
                    qkv_layer2(t, y_it)
                if has_z:
                    ff_down(s, it - 1)
                if has_x:
                    turn_xn(s, it)
                    q_and_k_layer1(s, it)
                if has_y:
                    pe.wait_ge(v2_ready[t], y_it + 1)
                    scores(t, 2 * y_it + 1)
                if has_x:
                    at_least(pe, out_ready[s], it)
                    scores(s, 2 * it)
                if has_y:
                    turn_max(t, 2 * y_it + 1)
                    scores_turned(t, 2 * y_it + 1)
                if has_x:
                    turn_max(s, 2 * it)
                    scores_turned(s, 2 * it)
                if has_y:
                    weigh_values(t, 2 * y_it + 1, v2)
                if has_x:
                    pe.wait_ge(v1_ready[s], it + 1)
                    weigh_values(s, 2 * it, v1)
                if has_y:
                    mix_heads(t, 2 * y_it + 1, wout_pad)
                if has_x:
                    mix_heads(s, 2 * it, wo_pad)
                if has_y:
                    turn_h2(t, y_it)
                    ff_up(t, y_it)

            def rows(it, first=False, last=False):
                half(it, 0, not last, None if first else it - 1, not first)
                if not last:
                    half(it, 1, True, it, not first)

            rows(0, first=True)
            with pe.Fori(1, NB) as it:
                rows(it)
            rows(NB, last=True)
            ff_down(1, NB - 1)

        @block.vector
        def _(dve):
            dve.memset(wo_pad[:, :, :], 0.0)
            dve.memset(wout_pad[:, :, :], 0.0)
            dve.memset(w3_pad[:, FC - 1, :], 0.0).then_inc(dve_const, 1)
            dve.wait_ge(bucket_loaded, 16)
            for e in range(E):
                ins = dve.tensor_scalar(onehot[:, e, :], bucket_i[:, :], float(e), None, ALU.is_equal)
            ins.then_inc(route, 1)
            dve.wait_ge(route, 1)
            dve.tensor_copy(onehot_b[:, :, :], onehot[:, :, :]).then_inc(onehot_ready, 1)
            dve.wait_ge(consts_ready, 1)
            dve.wait_ge(counts_ready, 1)
            flat = "p e b -> p (e b)"
            dve.tensor_tensor_scan(totals_scan[:, :, :].rearrange(flat), scan_keep[:, :, :].rearrange(flat),
                                   banks[7][:, 0:P], 0.0, ALU.mult, ALU.add).then_inc(route, 1)
            dve.wait_ge(route, 2)
            dve.tensor_tensor(over[:, :, :], totals_scan[:, :, B - 1:B].to_broadcast([P, E, B]),
                              tile_marks[:, :].unsqueeze(1).to_broadcast([P, E, B]), ALU.is_gt).then_inc(route, 1)
            dve.tensor_tensor(rank[:, :, :].rearrange(flat), totals_scan[:, :, :].rearrange(flat), banks[7][:, 0:P],
                              ALU.subtract).then_inc(route, 1)
            dve.wait_ge(route, 4)
            dve.tensor_tensor(rank[:, :, :].rearrange(flat), rank[:, :, :].rearrange(flat), banks[6][:, 0:P],
                              ALU.add).then_inc(route, 1)
            dve.tensor_reduce(tiles_e[:, :], over[:, :, :], AX.X, ALU.add).then_inc(route, 1)
            dve.wait_ge(route, 6)
            dve.tensor_tensor_scan(tiles_end[:, :], ones_e[:, :], tiles_e[:, :], 0.0, ALU.mult, ALU.add).then_inc(route, 1)
            dve.wait_ge(route, 7)
            dve.tensor_tensor(tiles_base[:, :], tiles_end[:, :], tiles_e[:, :], ALU.subtract).then_inc(route, 1)
            dve.tensor_tensor(past[:, :, :], tiles_end[0:1, :].unsqueeze(1).to_broadcast([1, NTILE, E]),
                              tile_ids[0:1, :].unsqueeze(2).to_broadcast([1, NTILE, E]), ALU.is_le).then_inc(route, 1)
            dve.wait_ge(route, 9)
            dve.scalar_tensor_tensor(rank[:, :, :], tiles_base[:, :].unsqueeze(2).to_broadcast([P, E, B]), float(P),
                                     rank[:, :, :], ALU.mult, ALU.add).then_inc(route, 1)
            dve.tensor_reduce(expert_f[:, :], past[:, :, :], AX.X, ALU.add).then_inc(route, 1)
            dve.wait_ge(route, 11)
            dve.tensor_tensor(rank[:, :, :], rank[:, :, :], onehot[:, :, :], ALU.mult).then_inc(route, 1)
            dve.tensor_scalar(expert_i[:, :], expert_f[:, :], float(E - 1), None, ALU.min).then_inc(experts_ready, 1)
            dve.wait_ge(route, 12)
            dve.tensor_reduce(slot_f[:, :], rank[:, :, :].rearrange("p e b -> p b e"), AX.X, ALU.add).then_inc(route, 1)
            dve.wait_ge(route, 13)
            dve.tensor_copy(slot_u[:, :], slot_f[:, :]).then_inc(slots_ready, 1)

            for t in (wq_pad, wq2_pad, wk2_pad):
                dve.memset(t[:, :, :], 0.0)
            for t in (w1_pad, w2_pad):
                ins = dve.memset(t[:, :, DFF:DFFP], 0.0)
            ins.then_inc(dve_const, 1)
            dve.wait_ge(dve_const, 2)
            dve.wait_ge(weights_loaded, 16 * (6 + 2 * G))
            dve.wait_ge(small_loaded, 16 * 8)

            def padded(t, k):
                return t[:, k, :].rearrange("p (h w) -> p h w", h=H)[:, :, 0:HD]

            def heads(t):
                return t.rearrange("p (h d) -> p h d", h=H)

            for k in range(KC):
                dve.tensor_copy(padded(wq_pad, k), heads(raw_q[:, k, :]))
                dve.tensor_scalar(padded(wq2_pad, k), heads(raw_qkv[:, k, 0:D]), g1_col[:, k:k + 1], None, ALU.mult)
                dve.tensor_scalar(padded(wk2_pad, k), heads(raw_qkv[:, k, D:2 * D]), g1_col[:, k:k + 1], None, ALU.mult)
                dve.tensor_scalar(wv2[:, k, :], raw_qkv[:, k, 2 * D:3 * D], g1_col[:, k:k + 1], None, ALU.mult)
                dve.tensor_scalar(w1_pad[:, k, 0:DFF], raw_ff[:, 0, k, :], g2_col[:, k:k + 1], None, ALU.mult)
                dve.tensor_scalar(w2_pad[:, k, 0:DFF], raw_ff[:, 1, k, :], g2_col[:, k:k + 1], None, ALU.mult)
            dve.wait_ge(rows_loaded, 32)
            dve.tensor_scalar(open_rows[:, :], pad_rows[:, :], -NEG, NEG, ALU.mult, ALU.add)
            dve.tensor_scalar(open_cols[:, :], pad_cols[:, :], -NEG, NEG, ALU.mult, ALU.add)
            dve.wait_ge(gates_ready, 1)
            dve.tensor_scalar(bias_row[:, :], bias_row[:, :], gates[:, 0:1], None, ALU.mult).then_inc(weights_ready, 1)
            dve.wait_ge(weights_ready, 1)

            dve.wait_ge(table_turned, 1)
            dve.tensor_copy(table_cols[:, :], banks[5][:, 0:NTILE]).then_inc(table_ready, 1)

            def copy_tiles(i):
                for j in range(UN):
                    dve.wait_ge(kv_in_psum[j], i + 1)
                    at_least(dve, kv_stored[j], 16 * i)
                    dve.tensor_copy(tile_kv[j][:, :], banks[2 + j][:, :]).then_inc(kv_copied[j], 1)

            turns(dve, NTILE // UN, copy_tiles)

            X_STEPS, Y_STEPS, Z_STEPS = 15, 8, 2
            ROW_STEPS = X_STEPS + Y_STEPS + Z_STEPS
            base, count = [0] * NS, [0] * NS

            def step(s, ins):
                count[s] += 1
                ins.then_inc(dve_step[s], 1)

            def last_step(s):
                dve.wait_ge(dve_step[s], base[s] + count[s])

            def moments(s, src):
                step(s, dve.bn_stats(stats[s][:, :], src))
                last_step(s)
                dve.memset(dve_held[:, :], 0.0)
                step(s, dve.bn_aggr(mean_var[s][:, :], stats[s][:, :]))
                last_step(s)
                step(s, dve.tensor_scalar(pow_in[s][:, 0:1], mean_var[s][:, 1:2], LN_EPS, None, ALU.add))
                last_step(s)
                dve.scalar_tensor_tensor(pow_in[s][:, 1:2], pow_in[s][:, 0:1], RMS_EPS, mean_var[s][:, 1:2],
                                         ALU.mult, ALU.add).then_inc(pow_asked[s], 1)

            def time_masks(s, it):
                b = NS * it + s
                t_row = time_rows[:, bass.ds(b * P, P)]
                t_col = time_cols[:, bass.ds(b, 1)]
                step(s, dve.scalar_tensor_tensor(neg_l[s][:, :], t_row, t_col, open_rows[:, bass.ds(b * P, P)],
                                                 ALU.is_le, ALU.mult))
                dve.tensor_scalar(neg_t[s][:, :], t_row, t_col, open_cols[:, bass.ds(b, 1)], ALU.is_ge, ALU.mult
                                  ).then_inc(masks_ready[s], 1)
                last_step(s)
                step(s, dve.tensor_reduce(any_open[s][:, :], neg_l[s][:, :], AX.X, ALU.max))

            def normalise_x(s, it):
                dve.wait_ge(pow_ready[s], 3 * it + 1)
                last_step(s)
                step(s, dve.scalar_tensor_tensor(q_rstd[s][:, :], any_open[s][:, :], 0.0, pow_out[s][:, 0:1],
                                                 ALU.is_equal, ALU.mult))
                last_step(s)
                dve.tensor_scalar(xn[s][:, :], x_sb[s][:, :], mean_var[s][:, 0:1], q_rstd[s][:, 0:1],
                                  ALU.subtract, ALU.mult).then_inc(xn_ready[s], 1)

            def maxima(s, u):
                dve.wait_ge(scores_ready[s], u + 1)
                for g in range(G):
                    ins = dve.tensor_reduce(max_pad[s][:, :, g, HD], bank(s, g)[:, :].rearrange("p (c m) -> p c m", c=C),
                                            AX.X, ALU.max)
                ins.then_inc(max_ready[s], 1)

            def join_max(s, u):
                dve.wait_ge(max_in_psum[s], u + 1)
                dve.tensor_tensor(q_aug[s][:, :, :], bank(s, 0)[:, :].rearrange("p (c m) -> p c m", c=C), q_t[s][:, :, :],
                                  ALU.add).then_inc(q_aug_ready[s], 1)

            def divide(s, u):
                dve.wait_ge(pv_ready[s], u + 1)
                step(s, dve.transpose(mixed_blocks[s][:, :, :].rearrange("p h w -> p (h w)"), bank(s, 0)[:, :]))
                last_step(s)
                step(s, dve.reciprocal(denom[s][:, :].unsqueeze(2), mixed_blocks[s][:, :, HD:HD + 1]))
                last_step(s)
                step(s, dve.tensor_tensor(attn_blocks[s][:, :, 0:HD], mixed_blocks[s][:, :, 0:HD],
                                          denom[s][:, :].unsqueeze(2).to_broadcast([P, H, HD]), ALU.mult))
                last_step(s)
                dve.transpose(attn_t[s][:, :, :].rearrange("p c m -> p (c m)"),
                              attn_blocks[s][:, :, :].rearrange("p h w -> p (h w)")).then_inc(attn_t_ready[s], 1)

            def residual1(s, it):
                dve.wait_ge(mixed_ready[s], 2 * it + 1)
                dve.wait_ge(x_bias_ready[s], it + 1)
                step(s, dve.scalar_tensor_tensor(x1[s][:, :], bank(s, 2)[:, 0:D], gates[:, 0:1], x_bias[s][:, :],
                                                 ALU.mult, ALU.add))
                last_step(s)
                dve.memset(dve_held[:, :], 0.0).then_inc(x1_ready[s], 1)

            def normalise_x1(s, it):
                dve.wait_ge(pow_ready[s], 3 * it + 2)
                step(s, dve.tensor_scalar(y[s][:, :], x1[s][:, :], mean_var[s][:, 0:1], pow_out[s][:, 0:1],
                                          ALU.subtract, ALU.mult))
                dve.tensor_scalar(h[s][:, :], x1[s][:, :], mean_var[s][:, 0:1], pow_out[s][:, 1:2],
                                  ALU.subtract, ALU.mult).then_inc(h_ready[s], 1)
                last_step(s)
                step(s, dve.tensor_tensor_reduce(junk[s][:, :], y[s][:, :], router_row[:, :], 1.0, 0.0, ALU.mult,
                                                 ALU.add, score[s][:, 0:1]))
                last_step(s)
                dve.tensor_copy(score_wide[s][:, :], score[s][:, 0:1].to_broadcast([P, P])).then_inc(score_ready[s], 1)

            def rank_masks(s, it):
                dve.wait_ge(score_in_psum[s], it + 1)
                row, col = bank(s, 0)[:, 0:P], score[s][:, 0:1]
                dve.scalar_tensor_tensor(mask_a[s][:, :], row, col, later_neg[:, :], ALU.is_le, ALU.mult)
                step(s, dve.tensor_scalar(mask_b[s][:, :], row, col, NEG, ALU.is_lt, ALU.mult))
                last_step(s)
                step(s, dve.tensor_tensor(neg_l[s][:, :], mask_a[s][:, :], mask_b[s][:, :], ALU.min))
                last_step(s)
                dve.scalar_tensor_tensor(mask_a[s][:, :], row, col, earlier_neg[:, :], ALU.is_ge, ALU.mult)
                step(s, dve.tensor_scalar(mask_b[s][:, :], row, col, NEG, ALU.is_gt, ALU.mult))
                last_step(s)
                dve.tensor_tensor(neg_t[s][:, :], mask_a[s][:, :], mask_b[s][:, :], ALU.min).then_inc(masks_ready[s], 1)

            def residual2(s, it):
                dve.wait_ge(mixed_ready[s], 2 * it + 2)
                step(s, dve.tensor_tensor(x2[s][:, :], bank(s, 2)[:, 0:D], y[s][:, :], ALU.add))
                last_step(s)
                step(s, dve.tensor_tensor_reduce(junk[s][:, :], x2[s][:, :], x2[s][:, :], 1.0 / D, 0.0, ALU.mult,
                                                 ALU.add, score[s][:, 0:1]))
                last_step(s)
                dve.tensor_scalar(pow_in[s][:, :], score[s][:, 0:1].to_broadcast([P, 2]), RMS_EPS, None, ALU.add
                                  ).then_inc(pow_asked[s], 1)

            def normalise_x2(s, it):
                dve.wait_ge(pow_ready[s], 3 * it + 3)
                dve.tensor_scalar(h2[s][:, :], x2[s][:, :], pow_out[s][:, 0:1], None, ALU.mult).then_inc(h2_ready[s], 1)

            def swiglu(s, it):
                dve.wait_ge(tanh_ready[s], it + 1)
                dve.scalar_tensor_tensor(silu_a[s][:, 0:512], tanh_a[s][:, 0:512], 1.0, bank(s, 1)[:, :], ALU.add, ALU.mult)
                step(s, dve.scalar_tensor_tensor(silu_a[s][:, 512:DFFP], tanh_a[s][:, 512:DFFP], 1.0,
                                                 bank(s, 2)[:, 0:DFFP - 512], ALU.add, ALU.mult))
                dve.wait_ge(ff_b_ready[s], it + 1)
                last_step(s)
                dve.scalar_tensor_tensor(hidden[s][:, 0:512], bank(s, 3)[:, :], 0.5, silu_a[s][:, 0:512], ALU.mult, ALU.mult)
                dve.scalar_tensor_tensor(hidden[s][:, 512:DFFP], bank(s, 0)[:, 0:DFFP - 512], 0.5, silu_a[s][:, 512:DFFP],
                                         ALU.mult, ALU.mult).then_inc(hidden_ready[s], 1)

            def residual3(s, it):
                dve.wait_ge(ff_ready[s], it + 1)
                step(s, dve.tensor_tensor(x3[s][:, :], bank(s, 3)[:, 0:D], x2[s][:, :], ALU.add))
                at_least(dve, out_stored[s], 16 * it)
                last_step(s)
                dve.scalar_tensor_tensor(y_out[s][:, :], x3[s][:, :], gates[:, 1:2], x1[s][:, :], ALU.mult, ALU.add
                                         ).then_inc(out_ready[s], 1)

            dve.wait_ge(consts_ready, 1 + 2 * NS)

            def half(it, s, has_x, y_it, has_z):
                t = 1 - s
                has_y = y_it is not None
                if has_z:
                    swiglu(s, it - 1)
                if has_x:
                    dve.wait_ge(x_loaded[s], 16 * it + 16)
                    moments(s, x_sb[s][:, :])
                    time_masks(s, it)
                if has_y:
                    rank_masks(t, y_it)
                if has_x:
                    normalise_x(s, it)
                if has_z:
                    residual3(s, it - 1)
                if has_y:
                    maxima(t, 2 * y_it + 1)
                    join_max(t, 2 * y_it + 1)
                if has_x:
                    maxima(s, 2 * it)
                    join_max(s, 2 * it)
                if has_y:
                    divide(t, 2 * y_it + 1)
                if has_x:
                    divide(s, 2 * it)
                if has_y:
                    residual2(t, y_it)
                    normalise_x2(t, y_it)
                if has_x:
                    residual1(s, it)
                    moments(s, x1[s][:, :])
                    normalise_x1(s, it)

            def rows(it, first=False, last=False):
                count[:] = [0, 0]
                if not first:
                    base[0], base[1] = ROW_STEPS * it - Z_STEPS, ROW_STEPS * it - Y_STEPS - Z_STEPS
                half(it, 0, not last, None if first else it - 1, not first)
                if not last:
                    half(it, 1, True, it, not first)
                    assert count[0] == ROW_STEPS - Z_STEPS * first, count
                    assert count[1] == (X_STEPS if first else ROW_STEPS), count

            rows(0, first=True)
            with dve.Fori(1, NB) as it:
                rows(it)
            rows(NB, last=True)
            swiglu(1, NB - 1)
            residual3(1, NB - 1)


_ORDER = ["x", "ctx", "times", "times_t", "bucket_t", "pad", "pad_t", "g_x", "g_f", "wq", "wkv", "wo", "bo",
          "w_router", "wqkv_t", "wout_t", "g1", "g2", "w1t", "w2t", "w3t"]


def kernel(x, ctx_1024, fside_BxS2_0, itok_BxS2_0_7, mask_BxS2_bf0, g_xattn, g_ffn, L0_xattn_Wq, L0_xattn_Wk_b,
           L0_xattn_Wv_b, L0_xattn_Wo, L0_xattn_bo, L0_ffn_w_router, L0_ffn_W_qkv, L0_ffn_W_out, L0_ffn_g1,
           L0_ffn_g2, L0_ffn_W1, L0_ffn_W2, L0_ffn_W3):
    import concourse.bacc as bacc
    from concourse.bass_utils import run_bass_kernel_spmd

    lay = lambda a: np.ascontiguousarray(a)
    wkv = np.concatenate([np.asarray(L0_xattn_Wk_b), np.asarray(L0_xattn_Wv_b)], axis=-1)
    wkv = wkv.reshape(E, KC, P, 2 * D).transpose(2, 1, 0, 3).reshape(P, KC * E * 2 * D)
    pad = lay(mask_BxS2_bf0)
    data = {
        "x": lay(x), "ctx": lay(ctx_1024).reshape(B * P, D), "times": lay(fside_BxS2_0),
        "times_t": lay(np.asarray(fside_BxS2_0).T), "bucket_t": lay(np.asarray(itok_BxS2_0_7).T),
        "pad": pad, "pad_t": lay(pad.T), "g_x": lay(g_xattn), "g_f": lay(g_ffn), "wq": lay(L0_xattn_Wq),
        "wkv": lay(wkv), "wo": lay(L0_xattn_Wo), "bo": lay(L0_xattn_bo), "w_router": lay(L0_ffn_w_router),
        "wqkv_t": lay(np.asarray(L0_ffn_W_qkv).T), "wout_t": lay(np.asarray(L0_ffn_W_out).T),
        "g1": lay(np.asarray(L0_ffn_g1).reshape(KC, P).T), "g2": lay(np.asarray(L0_ffn_g2).reshape(KC, P).T), "w1t": lay(np.asarray(L0_ffn_W1).T),
        "w2t": lay(np.asarray(L0_ffn_W2).T), "w3t": lay(np.asarray(L0_ffn_W3).T),
    }
    nc = bacc.Bacc("TRN2", target_bir_lowering=False, num_devices=1)
    arrays, args = {}, []
    for name in _ORDER:
        arrays[f"in_{name}"] = data[name]
        args.append(nc.dram_tensor(f"in_{name}", data[name].shape, mybir.dt.from_np(data[name].dtype),
                                   kind="ExternalInput").ap())
    args.append(nc.dram_tensor("out_0", (B, P, D), F32, kind="ExternalOutput").ap())
    build(nc, *args)
    r = run_bass_kernel_spmd(nc, [arrays], core_ids=[0])
    return r.results[0]["out_0"]
```

```python
import numpy as np
import concourse.bass as bass
from concourse import mybir
from contextlib import ExitStack

F32 = mybir.dt.float32
BF16 = mybir.dt.bfloat16
I32 = mybir.dt.int32
U32 = mybir.dt.uint32
U8 = mybir.dt.uint8
ALU = mybir.AluOpType
ACT = mybir.ActivationFunctionType
AX = mybir.AxisListType

P = 128
B = 16
D = 256
KC = D // P
H = 16
HD = D // H
G = 4
C = H // G
SLOT = P // G
E = 8
NTILE = B + E
DFF = 682
FC = 6
DFFP = FC * P
NEG = -float(2 ** 100)
SCALE = 1.0 / float(HD) ** 0.5
LN_EPS = 1e-5
RMS_EPS = 1e-6
NS = 2
NB = B // NS
UN = 4
TURNS = NTILE // UN
TILE_BITS = P.bit_length() - 1


def at_least(eng, sem, n):
    if not (isinstance(n, int) and n == 0):
        eng.wait_ge(sem, n)


def turns(eng, n, body):
    body(0)
    with eng.Fori(1, n) as i:
        body(i)


def build(nc, x, ctx_in, times, times_t, bucket_t, pad, pad_t, g_x, g_f, wq, wkv, wo, bo,
          w_router, wqkv_t, wout_t, g1, g2, w1t, w2t, w3t, out):
    stack = ExitStack()
    with stack:
        def sb(name, shape, dt=F32):
            return stack.enter_context(nc.sbuf_tensor(name, shape, dt))

        def pair(name, shape, dt=F32):
            return [sb(f"{name}{s}", shape, dt) for s in range(NS)]

        def sem(name):
            return stack.enter_context(nc.semaphore(name))

        def sems(name, n=NS):
            return [sem(f"{name}{s}") for s in range(n)]

        kv_sorted = nc.dram_tensor("kv_sorted", [NTILE * P, 2 * D], F32, kind="Internal").ap()

        ident = sb("ident", [P, P])
        ident_b = sb("ident_b", [P, P], BF16)
        ones_b = sb("ones_b", [P, P], BF16)
        before_b = sb("before_b", [P, P], BF16)
        later_neg = sb("later_neg", [P, P])
        earlier_neg = sb("earlier_neg", [P, P])
        neg_half = sb("neg_half", [P, 2])
        pool_held = sb("pool_held", [1, 1])
        dve_held = sb("dve_held", [1, 1])
        minus_one_rows = sb("minus_one_rows", [P, 1])
        tile_marks = sb("tile_marks", [P, B])
        tile_ids = sb("tile_ids", [P, NTILE])
        places = sb("places", [P, P])
        row_id = sb("row_id", [P, 1])
        scan_keep = sb("scan_keep", [P, E, B])
        ones_e = sb("ones_e", [P, E])
        wkv_sb = sb("wkv_sb", [P, KC, E, 2 * D])
        raw_q = sb("raw_q", [P, KC, D])
        wq_pad = sb("wq_pad", [P, KC, H * SLOT])
        wo_sb = sb("wo_sb", [P, KC, D])
        raw_qkv = sb("raw_qkv", [P, KC, 3 * D])
        wq2_pad = sb("wq2_pad", [P, KC, H * SLOT])
        wk2_pad = sb("wk2_pad", [P, KC, H * SLOT])
        wv2 = sb("wv2", [P, KC, D])
        wout_sb = sb("wout_sb", [P, KC, D])
        w1_pad = sb("w1_pad", [P, KC, DFFP])
        w2_pad = sb("w2_pad", [P, KC, DFFP])
        w3_pad = sb("w3_pad", [P, FC, D])
        g1_col = sb("g1_col", [P, KC])
        g2_col = sb("g2_col", [P, KC])
        router_row = sb("router_row", [P, D])
        bias_row = sb("bias_row", [P, D])
        gates = sb("gates", [P, 2])
        gates_raw = sb("gates_raw", [P, 2])
        time_rows = sb("time_rows", [P, B * P])
        time_cols = sb("time_cols", [P, B])
        pad_rows = sb("pad_rows", [P, B * P], U8)
        pad_cols = sb("pad_cols", [P, B], U8)
        open_rows = sb("open_rows", [P, B * P], BF16)
        open_cols = sb("open_cols", [P, B])

        bucket_i = sb("bucket_i", [P, B], I32)
        onehot = sb("onehot", [P, E, B])
        onehot_b = sb("onehot_b", [P, E, B], BF16)
        totals_scan = sb("totals_scan", [P, E, B])
        rank = sb("rank", [P, E, B])
        over = sb("over", [P, E, B])
        tiles_e = sb("tiles_e", [P, E])
        tiles_end = sb("tiles_end", [P, E])
        tiles_base = sb("tiles_base", [P, E])
        slot_f = sb("slot_f", [P, B])
        slot_u = sb("slot_u", [P, B], U32)
        past = sb("past", [1, NTILE, E])
        expert_f = sb("expert_f", [1, NTILE])
        expert_i = sb("expert_i", [1, NTILE], I32)
        slot_lo_u = sb("slot_lo_u", [P, B], U32)
        slot_hi_u = sb("slot_hi_u", [P, B], U32)
        slot_lo = sb("slot_lo", [P, B])
        slot_hi = sb("slot_hi", [P, B])
        table_cols = sb("table_cols", [P, NTILE])
        tile_index = sb("tile_index", [P, UN], U32)

        x_sb = pair("x_sb", [P, D])
        kv_index = pair("kv_index", [P, 1], U32)
        kv_raw = pair("kv_raw", [P, 2 * D])
        kv_held = pair("kv_held", [1, 1])
        k_pad = pair("k_pad", [P, H, SLOT])
        v1 = pair("v1", [P, H, SLOT])
        v2 = pair("v2", [P, H, SLOT])
        x_bias = pair("x_bias", [P, D])
        stats = pair("stats", [P, 6])
        mean_var = pair("mean_var", [P, 2])
        pow_in = pair("pow_in", [P, 2])
        pow_out = pair("pow_out", [P, 2])
        any_open = pair("any_open", [P, 1])
        q_rstd = pair("q_rstd", [P, 1])
        neg_l = pair("neg_l", [P, P], BF16)
        neg_t = pair("neg_t", [P, P], BF16)
        mask_a = pair("mask_a", [P, P])
        mask_b = pair("mask_b", [P, P])
        xn = pair("xn", [P, D])
        xn_t = pair("xn_t", [P, KC, P])
        q_t = pair("q_t", [P, C, P])
        k_t = pair("k_t", [P, C, P])
        q_aug = pair("q_aug", [P, C, P])
        max_pad = pair("max_pad", [P, C, G, SLOT])
        probs = pair("probs", [P, G, C, P])
        denom = pair("denom", [P, H])
        mixed_blocks = pair("mixed_blocks", [P, H, SLOT])
        attn_blocks = pair("attn_blocks", [P, KC, G, 2, HD])
        attn_t = pair("attn_t", [P, KC, P])
        x1 = pair("x1", [P, D])
        y = pair("y", [P, D])
        junk = pair("junk", [P, D])
        score = pair("score", [P, 1])
        score_wide = pair("score_wide", [P, P])
        h = pair("h", [P, D])
        h_t = pair("h_t", [P, KC, P])
        x2 = pair("x2", [P, D])
        h2 = pair("h2", [P, D])
        h2_t = pair("h2_t", [P, KC, P])
        probs_flat = [t[:, :, :, :].rearrange("p g c m -> p (g c m)") for t in probs]
        tanh_a = [t[:, 0:DFFP] for t in probs_flat]
        silu_a = tanh_a
        hidden = pair("hidden", [P, DFFP])
        tile_kv = [probs_flat[0][:, j * 2 * D:(j + 1) * 2 * D] for j in range(UN)]
        tile_ctx = [probs_flat[1][:, j * D:(j + 1) * D] for j in range(UN)]
        tile_ctx_t = [probs_flat[1][:, (UN + j) * D:(UN + j + 1) * D].rearrange("p (k m) -> p k m", k=KC)
                      for j in range(2)]
        at_place = probs_flat[0].bitcast(BF16)[:, 0:B * P].rearrange("p (b m) -> p b m", b=B)
        tile_parts = probs_flat[1].bitcast(BF16)[:, 0:3 * B * NTILE].rearrange("p (n b t) -> p n b t", n=3, b=B)
        in_tile = tile_parts[:, 0, :, :]
        id_of_tile = tile_parts[:, 1:3, :, :]
        x3 = pair("x3", [P, D])
        x4 = junk
        y_out = pair("y_out", [P, D])

        banks = [stack.enter_context(nc.psum_tensor(f"bank{i}", [P, 512], F32)) for i in range(8)]

        def bank(s, g):
            return banks[4 * s + g]

        bucket_loaded = sem("bucket_loaded")
        small_loaded = sem("small_loaded")
        rows_loaded = sem("rows_loaded")
        weights_loaded = sem("weights_loaded")
        last_loaded = sem("last_loaded")
        wkv_loaded = sem("wkv_loaded")
        pool_const = sem("pool_const")
        pool_carried = sem("pool_carried")
        consts_ready = sem("consts_ready")
        dve_const = sem("dve_const")
        prepared = sem("prepared")
        weights_ready = sem("weights_ready")
        route = sem("route")
        onehot_ready = sem("onehot_ready")
        counts_ready = sem("counts_ready")
        slots_ready = sem("slots_ready")
        experts_ready = sem("experts_ready")
        gates_ready = sem("gates_ready")
        routing_consts = sem("routing_consts")
        pads_ready = sem("pads_ready")
        places_ready = sem("places_ready")
        table_in_psum = sem("table_in_psum")
        table_ready = sem("table_ready")
        index_ready = sem("index_ready")
        ctx_gathered = sems("ctx_gathered", UN)
        ctx_turned = sems("ctx_turned", UN)
        ctx_t_ready = sems("ctx_t_ready", UN)
        kv_in_psum = sems("kv_in_psum", UN)
        kv_copied = sems("kv_copied", UN)
        kv_stored = sems("kv_stored", UN)

        x_loaded = sems("x_loaded")
        kv_index_ready = sems("kv_index_ready")
        kv_gathered = sems("kv_gathered")
        kv_carried = sems("kv_carried")
        k_pad_ready = sems("k_pad_ready")
        v1_ready = sems("v1_ready")
        v2_ready = sems("v2_ready")
        x_bias_ready = sems("x_bias_ready")
        dve_step = sems("dve_step")
        pow_asked = sems("pow_asked")
        pow_ready = sems("pow_ready")
        masks_ready = sems("masks_ready")
        xn_ready = sems("xn_ready")
        xn_in_psum = sems("xn_in_psum")
        xn_t_ready = sems("xn_t_ready")
        q_in_psum = sems("q_in_psum")
        k_in_psum = sems("k_in_psum")
        v_in_psum = sems("v_in_psum")
        q_t_ready = sems("q_t_ready")
        k_t_ready = sems("k_t_ready")
        scores_ready = sems("scores_ready")
        max_ready = sems("max_ready")
        max_in_psum = sems("max_in_psum")
        q_aug_ready = sems("q_aug_ready")
        scores_t_ready = sems("scores_t_ready")
        probs_ready = sems("probs_ready")
        pv_ready = sems("pv_ready")
        attn_t_ready = sems("attn_t_ready")
        x1_ready = sems("x1_ready")
        mixed_ready = sems("mixed_ready")
        score_ready = sems("score_ready")
        score_in_psum = sems("score_in_psum")
        h_ready = sems("h_ready")
        h_in_psum = sems("h_in_psum")
        h_t_ready = sems("h_t_ready")
        h2_ready = sems("h2_ready")
        h2_in_psum = sems("h2_in_psum")
        h2_t_ready = sems("h2_t_ready")
        ff_a_ready = sems("ff_a_ready")
        ff_b_ready = sems("ff_b_ready")
        tanh_ready = sems("tanh_ready")
        hidden_ready = sems("hidden_ready")
        ff_first_ready = sems("ff_first_ready")
        x3_ready = sems("x3_ready")
        ff_ready = sems("ff_ready")
        out_ready = sems("out_ready")
        out_stored = sems("out_stored")

        block = stack.enter_context(nc.Block())

        @block.sync
        def _(sp):
            sp.dma_start(bucket_i[:, :], bucket_t).then_inc(bucket_loaded, 16)
            sp.dma_start(wkv_sb[:, :, :, :].rearrange("p a e n -> p (a e n)"), wkv).then_inc(wkv_loaded, 16)

            def load_x(s, it):
                sp.dma_start(x_sb[s][:, :], x[bass.ds(NS * it + s, 1), :, :].rearrange("a p d -> (a p) d")
                             ).then_inc(x_loaded[s], 16)

            for s in range(NS):
                load_x(s, 0)
            def store_tiles(i):
                for j in range(UN):
                    sp.wait_ge(kv_copied[j], i + 1)
                    sp.dma_start(kv_sorted[bass.ds((UN * i + j) * P, P), :], tile_kv[j][:, :]).then_inc(kv_stored[j], 16)

            sp.wait_ge(ctx_gathered[UN - 1], 16)
            sp.dma_start(raw_q[:, :, :], wq.rearrange("(k p) n -> p k n", p=P)).then_inc(weights_loaded, 16)
            sp.dma_start(raw_qkv[:, :, :], wqkv_t.rearrange("(k p) n -> p k n", p=P)).then_inc(weights_loaded, 16)
            store_tiles(0)
            sp.dma_start(w1_pad[:, :, 0:DFF], w1t.rearrange("(k p) n -> p k n", p=P)).then_inc(weights_loaded, 16)
            sp.dma_start(pad_rows[:, :], pad.rearrange("(a b) t -> a (b t)", a=1).to_broadcast([P, B * P])).then_inc(rows_loaded, 16)
            store_tiles(1)
            sp.dma_start(w2_pad[:, :, 0:DFF], w2t.rearrange("(k p) n -> p k n", p=P)).then_inc(weights_loaded, 16)
            store_tiles(2)
            sp.dma_start(time_rows[:, :], times.rearrange("(a b) t -> a (b t)", a=1).to_broadcast([P, B * P])).then_inc(rows_loaded, 16)
            store_tiles(3)
            sp.dma_start(w3_pad[:, 0:FC - 1, :], w3t[0:(FC - 1) * P, :].rearrange("(k p) n -> p k n", p=P)).then_inc(last_loaded, 16)
            sp.wait_ge(dve_const, 1)
            sp.dma_start(w3_pad[0:DFF - (FC - 1) * P, FC - 1, :], w3t[(FC - 1) * P:DFF, :]).then_inc(last_loaded, 16)
            for dst, src in ((wo_sb, wo), (wout_sb, wout_t)):
                sp.dma_start(dst[:, :, :].rearrange("p k n -> p (k n)"), src).then_inc(last_loaded, 16)
            with sp.Fori(4, TURNS) as i:
                store_tiles(i)

            def half(it, s, has_x, has_z, more):
                if has_z:
                    sp.wait_ge(out_ready[s], it)
                    sp.dma_start(out[bass.ds(NS * (it - 1) + s, 1), :, :].rearrange("a p d -> (a p) d"), y_out[s][:, :]
                                 ).then_inc(out_stored[s], 16)
                if has_x and more:
                    sp.wait_ge(x_bias_ready[s], it + 1)
                    sp.wait_ge(xn_ready[s], it + 1)
                    load_x(s, it + 1)

            def rows(it, first=False, last=False, more=True):
                for s in range(NS):
                    half(it, s, not last, not first, more)

            rows(0, first=True)
            with sp.Fori(1, NB - 1) as it:
                rows(it)
            rows(NB - 1, more=False)
            rows(NB, last=True)
            for s in range(NS):
                sp.wait_ge(out_stored[s], 16 * NB)
            for j in range(UN):
                sp.wait_ge(kv_stored[j], 16 * TURNS)

        @block.gpsimd
        def _(pool):
            pool.memset(before_b[:, :], 1.0).then_inc(pool_const, 1)
            pool.memset(scan_keep[:, :, :], 1.0).then_inc(pool_const, 1)
            pool.memset(ones_b[:, :], 1.0)
            pool.memset(ones_e[:, :], 1.0)
            pool.wait_ge(pool_const, 2)
            pool.affine_select(out=before_b[:, :], in_=before_b[:, :], compare_op=ALU.is_gt, fill=0.0,
                               base=0, pattern=[[1, P]], channel_multiplier=-1)
            pool.affine_select(out=scan_keep[:, :, :], in_=scan_keep[:, :, :], compare_op=ALU.not_equal, fill=0.0,
                               base=0, pattern=[[0, E], [1, B]], channel_multiplier=0).then_inc(routing_consts, 1)
            pool.iota(row_id[:, :], pattern=[[0, 1]], base=0, channel_multiplier=1,
                      allow_small_or_imprecise_dtypes=True)
            pool.iota(tile_marks[:, :], pattern=[[P, B]], base=0, channel_multiplier=0,
                      allow_small_or_imprecise_dtypes=True)
            pool.iota(tile_ids[:, :], pattern=[[1, NTILE]], base=0, channel_multiplier=0,
                      allow_small_or_imprecise_dtypes=True)
            pool.iota(places[:, :], pattern=[[1, P]], base=0, channel_multiplier=0,
                      allow_small_or_imprecise_dtypes=True).then_inc(routing_consts, 1)
            pool.memset(ident[:, :], 0.0).then_inc(pool_const, 1)
            pool.memset(later_neg[:, :], NEG).then_inc(pool_const, 1)
            pool.memset(earlier_neg[:, :], NEG).then_inc(pool_const, 1)
            pool.memset(minus_one_rows[:, :], 0.0).then_inc(pool_const, 1)
            pool.memset(neg_half[:, :], -0.5)
            pool.wait_ge(pool_const, 6)
            pool.affine_select(out=ident[:, :], in_=ident[:, :], compare_op=ALU.not_equal, fill=1.0,
                               base=0, pattern=[[-1, P]], channel_multiplier=1).then_inc(pool_const, 1)
            pool.affine_select(out=later_neg[:, :], in_=later_neg[:, :], compare_op=ALU.is_gt, fill=0.0,
                               base=0, pattern=[[1, P]], channel_multiplier=-1)
            pool.affine_select(out=earlier_neg[:, :], in_=earlier_neg[:, :], compare_op=ALU.is_gt, fill=0.0,
                               base=0, pattern=[[-1, P]], channel_multiplier=1)
            for g in range(G):
                ins = pool.affine_select(out=minus_one_rows[:, :], in_=minus_one_rows[:, :], compare_op=ALU.not_equal,
                                         fill=-1.0, base=-(SLOT * g + HD), pattern=[[0, 1]], channel_multiplier=1)
                ins.then_inc(pool_const, 1)
                pool.wait_ge(pool_const, 8 + g)
            pool.tensor_copy(ident_b[:, :], ident[:, :]).then_inc(consts_ready, 1)
            for s in range(NS):
                pool.memset(k_pad[s][:, :, :], 0.0)
                pool.memset(v1[s][:, :, :], 0.0)
                pool.memset(v2[s][:, :, :], 0.0)
                pool.memset(max_pad[s][:, :, :, :], 0.0).then_inc(pads_ready, 1)
            pool.wait_ge(pads_ready, NS)
            for s in range(NS):
                pool.memset(v1[s][:, :, HD:HD + 1], 1.0)
                pool.memset(v2[s][:, :, HD:HD + 1], 1.0).then_inc(pads_ready, 1)
            pool.wait_ge(pads_ready, 2 * NS)
            pool.wait_ge(table_ready, 1)
            def hold():
                pool.wait_ge(table_ready, 1)

            def carry(n):
                at_least(pool, pool_carried, n)
                pool.tensor_tensor(pool_held[:, :], neg_half[0:1, 0:1], neg_half[0:1, 0:1], ALU.add).then_inc(pool_carried, 1)

            def gather_tiles(i):
                hold()
                for j in range(UN):
                    at_least(pool, ctx_gathered[j], 16 * i)
                pool.tensor_copy(tile_index[:, :], table_cols[:, bass.ds(UN * i, UN)]).then_inc(index_ready, 1)
                for j in range(UN):
                    pool.wait_ge(index_ready, i + 1)
                    at_least(pool, ctx_turned[j], i)
                    carry(UN * i + j)
                    pool.indirect_dma_start(out=tile_ctx[j][:, :], out_offset=None, in_=ctx_in,
                                            in_offset=bass.IndirectOffsetOnAxis(ap=tile_index[:, j:j + 1], axis=0)
                                            ).then_inc(ctx_gathered[j], 16)

            turns(pool, TURNS, gather_tiles)

            def gather_kv(s, it):
                pool.tensor_copy(kv_index[s][:, :], slot_u[:, bass.ds(NS * it + s, 1)]).then_inc(kv_index_ready[s], 1)
                pool.wait_ge(kv_index_ready[s], it + 1)
                carry(NTILE + NS * it + s)
                pool.indirect_dma_start(out=kv_raw[s][:, :], out_offset=None, in_=kv_sorted,
                                        in_offset=bass.IndirectOffsetOnAxis(ap=kv_index[s][:, 0:1], axis=0)
                                        ).then_inc(kv_gathered[s], 16)

            def spread_kv(s, it):
                pool.wait_ge(kv_gathered[s], 16 * it + 16)
                at_least(pool, k_in_psum[s], 2 * it)
                at_least(pool, pv_ready[s], 2 * it)
                at_least(pool, kv_carried[s], it)
                pool.tensor_tensor(kv_held[s][:, :], neg_half[0:1, 0:1], neg_half[0:1, 0:1], ALU.add).then_inc(kv_carried[s], 1)
                pool.tensor_copy(k_pad[s][:, :, 0:HD], kv_raw[s][:, 0:D].rearrange("p (h d) -> p h d", h=H)
                                 ).then_inc(k_pad_ready[s], 1)
                pool.tensor_copy(v1[s][:, :, 0:HD], kv_raw[s][:, D:2 * D].rearrange("p (h d) -> p h d", h=H)
                                 ).then_inc(v1_ready[s], 1)

            def add_bias(s, it):
                pool.wait_ge(x_loaded[s], 16 * it + 16)
                at_least(pool, x1_ready[s], it)
                pool.tensor_tensor(x_bias[s][:, :], x_sb[s][:, :], bias_row[:, :], ALU.add).then_inc(x_bias_ready[s], 1)

            def power(s, it, k):
                if k == 0:
                    at_least(pool, h2_ready[s], it)
                pool.wait_ge(pow_asked[s], 3 * it + k + 1)
                pool.tensor_tensor(pow_out[s][:, :], pow_in[s][:, :], neg_half[:, :], ALU.pow).then_inc(pow_ready[s], 1)

            def keys_and_values(s, it, more):
                spread_kv(s, it)
                if more:
                    hold()
                    pool.wait_ge(v1_ready[s], it + 1)
                    gather_kv(s, it + 1)

            power(0, 0, 0)
            hold()
            for j in range(UN):
                pool.wait_ge(kv_stored[j], 16 * TURNS)
            for s in range(NS):
                gather_kv(s, 0)
            pool.wait_ge(weights_ready, 1)
            keys_and_values(0, 0, True)
            add_bias(0, 0)

            def half(it, s, has_x, y_it, f_it, more):
                t = 1 - s
                if f_it is not None:
                    keys_and_values(t, f_it, more)
                if y_it is not None:
                    power(t, y_it, 2)
                if f_it is not None:
                    power(t, f_it, 0)
                if has_x:
                    power(s, it, 1)
                if f_it is not None:
                    add_bias(t, f_it)

            def rows(it, first=False, left=2):
                half(it, 0, left >= 0, None if first else it - 1, it if left >= 0 else None, left >= 1)
                if left >= 0:
                    half(it, 1, True, it, it + 1 if left >= 1 else None, left >= 2)

            rows(0, first=True)
            with pool.Fori(1, NB - 2) as it:
                rows(it)
            rows(NB - 2, left=1)
            rows(NB - 1, left=0)
            rows(NB, left=-1)

        @block.scalar
        def _(act):
            act.dma_start(gates_raw[:, 0:1], g_x.rearrange("(a n) -> a n", a=1).to_broadcast([P, 1])).then_inc(small_loaded, 16)
            act.dma_start(gates_raw[:, 1:2], g_f.rearrange("(a n) -> a n", a=1).to_broadcast([P, 1])).then_inc(small_loaded, 16)
            act.dma_start(g1_col[:, :], g1).then_inc(small_loaded, 16)
            act.dma_start(g2_col[:, :], g2).then_inc(small_loaded, 16)
            act.dma_start(time_cols[:, :], times_t).then_inc(small_loaded, 16)
            act.dma_start(pad_cols[:, :], pad_t).then_inc(small_loaded, 16)
            act.dma_start(router_row[:, :], w_router.rearrange("(a n) -> a n", a=1).to_broadcast([P, D])).then_inc(small_loaded, 16)
            act.dma_start(bias_row[:, :], bo.rearrange("(a n) -> a n", a=1).to_broadcast([P, D])).then_inc(small_loaded, 16)
            act.wait_ge(small_loaded, 16 * 8)
            act.activation(gates[:, :], gates_raw[:, :], ACT.Tanh).then_inc(gates_ready, 1)

            def copy_tiles(i):
                for j in range(UN):
                    act.wait_ge(ctx_turned[j], i + 1)
                    act.activation(tile_ctx_t[j % 2][:, :, :], banks[j % 2][:, 0:D].rearrange("p (k m) -> p k m", k=KC),
                                   ACT.Copy).then_inc(ctx_t_ready[j], 1)

            turns(act, TURNS, copy_tiles)

            def three(t):
                return t.rearrange("p (k m) -> p k m", k=KC)

            def copy_xn(s, it):
                act.wait_ge(xn_in_psum[s], it + 1)
                act.activation(xn_t[s][:, :, :], three(bank(s, 0)[:, 0:D]), ACT.Copy).then_inc(xn_t_ready[s], 1)

            def copy_q(s, u):
                act.wait_ge(q_in_psum[s], u + 1)
                act.activation(q_t[s][:, :, :], bank(s, 1)[:, :].rearrange("p (c m) -> p c m", c=C),
                               ACT.Copy).then_inc(q_t_ready[s], 1)

            def copy_k(s, u, src):
                act.wait_ge(k_in_psum[s], u + 1)
                act.activation(k_t[s][:, :, :], src[:, :].rearrange("p (c m) -> p c m", c=C),
                               ACT.Identity, bias=minus_one_rows[:, 0:1]).then_inc(k_t_ready[s], 1)

            def copy_v(s, it):
                act.wait_ge(v_in_psum[s], it + 1)
                act.activation(v2[s][:, :, 0:HD], bank(s, 3)[:, 0:D].rearrange("p (h d) -> p h d", h=H),
                               ACT.Copy).then_inc(v2_ready[s], 1)

            def exponentials(s, u):
                act.wait_ge(scores_t_ready[s], u + 1)
                for g in (3, 0, 1, 2):
                    act.activation(probs[s][:, g, :, :], bank(s, g)[:, :].rearrange("p (c m) -> p c m", c=C),
                                   ACT.Exp, scale=SCALE).then_inc(probs_ready[s], 1)

            def copy_h(s, it):
                act.wait_ge(h_in_psum[s], it + 1)
                act.activation(h_t[s][:, :, :], three(bank(s, 3)[:, 0:D]), ACT.Copy).then_inc(h_t_ready[s], 1)

            def copy_h2(s, it):
                act.wait_ge(h2_in_psum[s], it + 1)
                act.activation(h2_t[s][:, :, :], three(bank(s, 0)[:, 0:D]), ACT.Copy).then_inc(h2_t_ready[s], 1)

            def tanh_half(s, it):
                act.wait_ge(ff_a_ready[s], it + 1)
                act.activation(tanh_a[s][:, 0:512], bank(s, 1)[:, :], ACT.Tanh, scale=0.5)
                act.activation(tanh_a[s][:, 512:DFFP], bank(s, 2)[:, 0:DFFP - 512], ACT.Tanh, scale=0.5
                               ).then_inc(tanh_ready[s], 1)

            def half(it, s, has_x, y_it, f_it):
                t = 1 - s
                if y_it is not None:
                    copy_q(t, 2 * y_it + 1)
                if has_x:
                    copy_xn(s, it)
                if y_it is not None:
                    copy_k(t, 2 * y_it + 1, bank(t, 2))
                    copy_v(t, y_it)
                if has_x:
                    copy_q(s, 2 * it)
                if has_x and y_it is None:
                    copy_k(s, 2 * it, bank(s, 2))
                if y_it is not None:
                    exponentials(t, 2 * y_it + 1)
                if has_x:
                    exponentials(s, 2 * it)
                if y_it is not None:
                    copy_h2(t, y_it)
                if f_it is not None:
                    copy_k(t, 2 * f_it, bank(s, 1))
                if y_it is not None:
                    tanh_half(t, y_it)
                if has_x:
                    copy_h(s, it)

            def rows(it, first=False, left=1):
                half(it, 0, left >= 0, None if first else it - 1, it if left >= 0 else None)
                if left >= 0:
                    half(it, 1, True, it, it + 1 if left >= 1 else None)

            rows(0, first=True)
            with act.Fori(1, NB - 1) as it:
                rows(it)
            rows(NB - 1, left=0)
            rows(NB, left=-1)

        @block.tensor
        def _(pe):
            pe.wait_ge(routing_consts, 1)
            pe.wait_ge(onehot_ready, 1)
            pe.matmul(banks[6][:, 0:P], before_b[:, :], onehot_b[:, :, :], start=True, stop=True)
            pe.matmul(banks[7][:, 0:P], ones_b[:, :], onehot_b[:, :, :], start=True, stop=True).then_inc(counts_ready, 1)
            for b in range(B):
                if b % 4 == 0:
                    pe.wait_ge(places_ready, b // 4 + 1)
                ins = pe.matmul(banks[5][:, 0:2 * NTILE].rearrange("p (n t) -> p n t", n=2), at_place[:, b, :],
                                id_of_tile[:, :, b, :], start=(b == 0), stop=(b == B - 1))
            ins.then_inc(table_in_psum, 1)

            def turn(dst, src):
                for k in range(KC):
                    ins = pe.transpose(dst[:, k * P:(k + 1) * P], src[:, k * P:(k + 1) * P], ident[:, :])
                return ins

            def turn_tile(j, i):
                pe.wait_ge(ctx_gathered[j], 16 * i + 16)
                turn(banks[j % 2], tile_ctx[j]).then_inc(ctx_turned[j], 1)

            def project_tile(j, i):
                expert = nc.tensor.value_load(expert_i[0:1, bass.ds(UN * i + j, 1)], min_val=0, max_val=E - 1)
                pe.wait_ge(ctx_t_ready[j], i + 1)
                at_least(pe, kv_copied[j], i)
                for k in range(KC):
                    ins = pe.matmul(banks[2 + j][:, :], tile_ctx_t[j % 2][:, k, :],
                                    wkv_sb[:, k, bass.ds(expert, 1), :].rearrange("p a n -> p (a n)"),
                                    start=(k == 0), stop=(k == KC - 1))
                ins.then_inc(kv_in_psum[j], 1)

            pe.wait_ge(wkv_loaded, 16)
            pe.wait_ge(consts_ready, 1)
            pe.wait_ge(experts_ready, 1)
            pe.wait_ge(table_ready, 1)
            def tiles(i, last=False):
                for j in range(UN):
                    if j + 1 < UN:
                        if j > 0:
                            pe.wait_ge(ctx_t_ready[j - 1], i + 1)
                        elif not (isinstance(i, int) and i == 0):
                            pe.wait_ge(ctx_t_ready[UN - 1], i)
                        turn_tile(j + 1, i)
                    elif not last:
                        pe.wait_ge(ctx_t_ready[j - 1], i + 1)
                        turn_tile(0, i + 1)
                    project_tile(j, i)

            turn_tile(0, 0)
            tiles(0)
            with pe.Fori(1, TURNS - 1) as i:
                tiles(i)
            tiles(TURNS - 1, last=True)

            def turn_xn(s, it):
                pe.wait_ge(xn_ready[s], it + 1)
                turn(bank(s, 0), xn[s]).then_inc(xn_in_psum[s], 1)

            def project_pad(dst, w, act_t, chunks=range(C)):
                for c in chunks:
                    for k in range(KC):
                        ins = pe.matmul(dst[:, c * P:(c + 1) * P], w[:, k, c * P:(c + 1) * P], act_t[:, k, :],
                                        start=(k == 0), stop=(k == KC - 1))
                return ins

            def turn_k(s, it, dst):
                pe.wait_ge(k_pad_ready[s], it + 1)
                for c in range(C):
                    ins = pe.transpose(dst[:, c * P:(c + 1) * P],
                                       k_pad[s][:, G * c:G * c + G, :].rearrange("p g w -> p (g w)"), ident[:, :])
                ins.then_inc(k_in_psum[s], 1)

            def q_layer1(s, it, chunks):
                pe.wait_ge(xn_t_ready[s], it + 1)
                ins = project_pad(bank(s, 1), wq_pad, xn_t[s], chunks)
                if chunks[-1] == C - 1:
                    ins.then_inc(q_in_psum[s], 1)

            def head(t, c, g):
                return t[SLOT * g:SLOT * g + SLOT, c, :]

            def add_mask(s, g, half, mask):
                pe.matmul(bank(s, g)[:, half * 2 * P:(half + 1) * 2 * P].rearrange("p (c m) -> p c m", c=2), ident_b[:, :],
                          mask[:, :].unsqueeze(1).to_broadcast([P, 2, P]), start=True, stop=False, skip_group_check=True)

            def products(s, c, a, b):
                for g in range(G):
                    ins = pe.matmul(bank(s, g)[:, c * P:(c + 1) * P], head(a[s], c, g), head(b[s], c, g),
                                    start=False, stop=True, skip_group_check=True)
                return ins

            def scores_first(s, u, z_count=0):
                pe.wait_ge(masks_ready[s], u + 1)
                pe.wait_ge(q_t_ready[s], u + 1)
                pe.wait_ge(k_t_ready[s], u + 1)
                for g in range(G):
                    if g == G - 1:
                        at_least(pe, x3_ready[s], z_count)
                    add_mask(s, g, 0, neg_l[s])
                for c in (0, 1):
                    products(s, c, q_t, k_t)
                for g in range(G):
                    add_mask(s, g, 1, neg_l[s])

            def scores_chunk(s, c):
                ins = products(s, c, q_t, k_t)
                if c == C - 1:
                    ins.then_inc(scores_ready[s], 1)

            def turn_max(s, u):
                pe.wait_ge(max_ready[s], u + 1)
                for c in range(C):
                    ins = pe.transpose(bank(s, 0)[:, c * P:(c + 1) * P],
                                       max_pad[s][:, c, :, :].rearrange("p g w -> p (g w)"), ident[:, :])
                ins.then_inc(max_in_psum[s], 1)

            def scores_turned_first(s, u):
                for g in (1, 2, 3, 0):
                    if g == 0:
                        pe.wait_ge(q_aug_ready[s], u + 1)
                    add_mask(s, g, 0, neg_t[s])
                for c in (0, 1):
                    products(s, c, k_t, q_aug)

            def scores_turned_second(s):
                for g in range(G):
                    add_mask(s, g, 1, neg_t[s])
                for c in (2, 3):
                    scores_turned_chunk(s, c)

            def scores_turned_chunk(s, c):
                ins = products(s, c, k_t, q_aug)
                if c == C - 1:
                    ins.then_inc(scores_t_ready[s], 1)

            def weigh_values(s, u, v):
                pe.wait_ge(probs_ready[s], G * u + G)
                for c in range(C):
                    for g in range(G):
                        ins = pe.matmul(bank(s, 0)[SLOT * g:SLOT * g + SLOT, c * P:(c + 1) * P], v[s][:, G * c + g, :],
                                        probs[s][:, g, c, :], start=True, stop=True)
                ins.then_inc(pv_ready[s], 1)

            def mix_heads(s, u, w):
                for k in range(KC):
                    pe.wait_ge(attn_t_ready[s], 2 * u + 1 + k)
                    ins = pe.matmul(bank(s, 2)[:, 0:D], attn_t[s][:, k, :], w[:, k, :], start=(k == 0), stop=(k == KC - 1))
                ins.then_inc(mixed_ready[s], 1)

            def turn_score(s, it):
                pe.wait_ge(score_ready[s], it + 1)
                pe.transpose(bank(s, 0)[:, 0:P], score_wide[s][:, :], ident[:, :]).then_inc(score_in_psum[s], 1)

            def turn_h(s, it):
                pe.wait_ge(h_ready[s], it + 1)
                turn(bank(s, 3), h[s]).then_inc(h_in_psum[s], 1)

            def q_layer2(s, it):
                pe.wait_ge(h_t_ready[s], it + 1)
                project_pad(bank(s, 1), wq2_pad, h_t[s]).then_inc(q_in_psum[s], 1)

            def k_layer2(s, chunks):
                ins = project_pad(bank(s, 2), wk2_pad, h_t[s], chunks)
                if chunks[-1] == C - 1:
                    ins.then_inc(k_in_psum[s], 1)

            def v_layer2(s, it):
                for k in range(KC):
                    ins = pe.matmul(bank(s, 3)[:, 0:D], h_t[s][:, k, :], wv2[:, k, :], start=(k == 0), stop=(k == KC - 1))
                ins.then_inc(v_in_psum[s], 1)

            def turn_h2(s, it):
                pe.wait_ge(h2_ready[s], it + 1)
                turn(bank(s, 0), h2[s]).then_inc(h2_in_psum[s], 1)

            def ff_place(s, n, first, second):
                return (bank(s, first)[:, n * P:(n + 1) * P] if n < 4 else bank(s, second)[:, (n - 4) * P:(n - 3) * P])

            def ff_up(s, w, first, second, chunks, done=None):
                for n in chunks:
                    for k in range(KC):
                        ins = pe.matmul(ff_place(s, n, first, second), w[:, k, n * P:(n + 1) * P], h2_t[s][:, k, :],
                                        start=(k == 0), stop=(k == KC - 1))
                if done is not None:
                    ins.then_inc(done[s], 1)

            def ff_down(s, it, bk, chunks, done=None):
                pe.wait_ge(hidden_ready[s], it + 1)
                for n in chunks:
                    ins = pe.matmul(bk[:, 0:D], hidden[s][:, n * P:(n + 1) * P], w3_pad[:, n, :],
                                    start=(n in (FF_FIRST[0], FF_REST[0])), stop=(n in (FF_FIRST[-1], FF_REST[-1])),
                                    skip_group_check=True)
                if done is not None:
                    ins.then_inc(done[s], 1)

            pe.wait_ge(weights_ready, 1)
            pe.wait_ge(pads_ready, 2 * NS)
            FF_FIRST, FF_REST = (0, 1), (2, 3, 4, 5)

            def half(it, s, has_x, y_it, has_z, f_it):
                t = 1 - s
                has_y = y_it is not None
                u, v = 2 * it, (2 * y_it + 1 if has_y else None)
                if has_y and has_x:
                    pe.wait_ge(k_t_ready[s], u + 1)
                if has_y:
                    q_layer2(t, y_it)
                    turn_score(t, y_it)
                    k_layer2(t, (0,))
                if has_z:
                    pe.wait_ge(hidden_ready[s], it)
                if has_x:
                    turn_xn(s, it)
                if has_y:
                    k_layer2(t, (1, 2, 3))
                    v_layer2(t, y_it)
                if has_x and has_y:
                    q_layer1(s, it, (0, 1, 2) if has_z else (0, 1))
                elif has_x:
                    q_layer1(s, it, (0, 1, 2, 3))
                    turn_k(s, it, bank(s, 2))
                if has_y:
                    pe.wait_ge(v2_ready[t], y_it + 1)
                    scores_first(t, v)
                if has_x and has_y:
                    q_layer1(s, it, (3,) if has_z else (2,))
                if has_z:
                    ff_down(s, it - 1, bank(s, 3), (0,))
                if has_y:
                    scores_chunk(t, 2)
                if has_z:
                    ff_down(s, it - 1, bank(s, 3), (1,), ff_first_ready)
                elif has_x and has_y:
                    q_layer1(s, it, (3,))
                if has_y:
                    scores_chunk(t, 3)
                if has_z and not has_x:
                    ff_down(s, it - 1, bank(s, 2), FF_REST, ff_ready)
                if has_x:
                    scores_first(s, u, it if has_z else 0)
                    scores_chunk(s, 2)
                if has_y:
                    turn_max(t, v)
                if has_x:
                    scores_chunk(s, 3)
                if has_y:
                    scores_turned_first(t, v)
                    for g in range(G):
                        add_mask(t, g, 1, neg_t[t])
                    scores_turned_chunk(t, 2)
                if has_x:
                    turn_max(s, u)
                if has_y:
                    scores_turned_chunk(t, 3)
                if has_x:
                    scores_turned_first(s, u)
                if has_z and has_x:
                    pe.wait_ge(probs_ready[t], G * v + 1)
                    ff_down(s, it - 1, bank(t, 3), (2,))
                if has_y:
                    weigh_values(t, v, v2)
                if has_x:
                    scores_turned_second(s)
                if has_y:
                    mix_heads(t, v, wout_sb)
                if has_z and has_x:
                    ff_down(s, it - 1, bank(t, 3), (3, 4))
                if has_x:
                    pe.wait_ge(v1_ready[s], it + 1)
                    weigh_values(s, u, v1)
                if has_y:
                    turn_h2(t, y_it)
                if has_z and has_x:
                    ff_down(s, it - 1, bank(t, 3), (5,), ff_ready)
                if f_it is not None:
                    turn_k(t, f_it, bank(s, 1))
                if has_y:
                    pe.wait_ge(h2_t_ready[t], y_it + 1)
                    ff_up(t, w1_pad, 1, 2, range(3))
                if has_x:
                    mix_heads(s, u, wo_sb)
                if has_y:
                    ff_up(t, w1_pad, 1, 2, range(3, FC), ff_a_ready)
                    if has_z:
                        pe.wait_ge(out_ready[s], it)
                    ff_up(t, w2_pad, 3, 0, range(5))
                if has_x:
                    turn_h(s, it)
                if has_y:
                    ff_up(t, w2_pad, 3, 0, range(5, FC), ff_b_ready)

            def rows(it, first=False, left=1):
                half(it, 0, left >= 0, None if first else it - 1, not first, it if left >= 0 else None)
                if left >= 0:
                    half(it, 1, True, it, not first, it + 1 if left >= 1 else None)

            rows(0, first=True)
            with pe.Fori(1, NB - 1) as it:
                rows(it)
            rows(NB - 1, left=0)
            rows(NB, left=-1)
            ff_down(1, NB - 1, bank(1, 3), FF_FIRST, ff_first_ready)
            pe.wait_ge(x3_ready[0], NB)
            ff_down(1, NB - 1, bank(0, 3), FF_REST, ff_ready)

        @block.vector
        def _(dve):
            dve.memset(w3_pad[:, FC - 1, :], 0.0).then_inc(dve_const, 1)
            dve.wait_ge(bucket_loaded, 16)
            for e in range(E):
                ins = dve.tensor_scalar(onehot[:, e, :], bucket_i[:, :], float(e), None, ALU.is_equal)
            ins.then_inc(route, 1)
            dve.wait_ge(route, 1)
            dve.tensor_copy(onehot_b[:, :, :], onehot[:, :, :]).then_inc(onehot_ready, 1)
            dve.wait_ge(routing_consts, 2)
            dve.wait_ge(counts_ready, 1)
            flat = "p e b -> p (e b)"
            dve.tensor_tensor_scan(totals_scan[:, :, :].rearrange(flat), scan_keep[:, :, :].rearrange(flat),
                                   banks[7][:, 0:P], 0.0, ALU.mult, ALU.add).then_inc(route, 1)
            dve.wait_ge(route, 2)
            dve.tensor_tensor(over[:, :, :], totals_scan[:, :, B - 1:B].to_broadcast([P, E, B]),
                              tile_marks[:, :].unsqueeze(1).to_broadcast([P, E, B]), ALU.is_gt).then_inc(route, 1)
            dve.tensor_tensor(rank[:, :, :].rearrange(flat), totals_scan[:, :, :].rearrange(flat), banks[7][:, 0:P],
                              ALU.subtract).then_inc(route, 1)
            dve.wait_ge(route, 4)
            dve.tensor_tensor(rank[:, :, :].rearrange(flat), rank[:, :, :].rearrange(flat), banks[6][:, 0:P],
                              ALU.add).then_inc(route, 1)
            dve.tensor_reduce(tiles_e[:, :], over[:, :, :], AX.X, ALU.add).then_inc(route, 1)
            dve.wait_ge(route, 6)
            dve.tensor_tensor_scan(tiles_end[:, :], ones_e[:, :], tiles_e[:, :], 0.0, ALU.mult, ALU.add).then_inc(route, 1)
            dve.wait_ge(route, 7)
            dve.tensor_tensor(tiles_base[:, :], tiles_end[:, :], tiles_e[:, :], ALU.subtract).then_inc(route, 1)
            dve.tensor_tensor(past[:, :, :], tiles_end[0:1, :].unsqueeze(1).to_broadcast([1, NTILE, E]),
                              tile_ids[0:1, :].unsqueeze(2).to_broadcast([1, NTILE, E]), ALU.is_le).then_inc(route, 1)
            dve.wait_ge(route, 9)
            dve.scalar_tensor_tensor(rank[:, :, :], tiles_base[:, :].unsqueeze(2).to_broadcast([P, E, B]), float(P),
                                     rank[:, :, :], ALU.mult, ALU.add).then_inc(route, 1)
            dve.tensor_reduce(expert_f[:, :], past[:, :, :], AX.X, ALU.add).then_inc(route, 1)
            dve.wait_ge(route, 11)
            dve.tensor_tensor(rank[:, :, :], rank[:, :, :], onehot[:, :, :], ALU.mult).then_inc(route, 1)
            dve.tensor_scalar(expert_i[:, :], expert_f[:, :], float(E - 1), None, ALU.min).then_inc(experts_ready, 1)
            dve.wait_ge(route, 12)
            dve.tensor_reduce(slot_f[:, :], rank[:, :, :].rearrange("p e b -> p b e"), AX.X, ALU.add).then_inc(route, 1)
            dve.wait_ge(route, 13)
            dve.tensor_copy(slot_u[:, :], slot_f[:, :]).then_inc(slots_ready, 1)
            dve.wait_ge(slots_ready, 1)
            dve.tensor_scalar(slot_hi_u[:, :], slot_u[:, :], TILE_BITS, None, ALU.logical_shift_right).then_inc(route, 1)
            dve.tensor_scalar(slot_lo_u[:, :], slot_u[:, :], P - 1, None, ALU.bitwise_and).then_inc(route, 1)
            dve.wait_ge(route, 15)
            dve.tensor_copy(slot_hi[:, :], slot_hi_u[:, :]).then_inc(route, 1)
            dve.tensor_copy(slot_lo[:, :], slot_lo_u[:, :]).then_inc(route, 1)
            dve.wait_ge(route, 17)
            dve.tensor_tensor(in_tile, slot_hi[:, :].unsqueeze(2).to_broadcast([P, B, NTILE]),
                              tile_ids[:, :].unsqueeze(1).to_broadcast([P, B, NTILE]), ALU.is_equal).then_inc(route, 1)
            dve.wait_ge(route, 18)
            dve.tensor_tensor(id_of_tile[:, 0, :, :], in_tile, tile_marks[:, :].unsqueeze(2).to_broadcast([P, B, NTILE]),
                              ALU.mult)
            dve.tensor_scalar(id_of_tile[:, 1, :, :], in_tile, row_id[:, 0:1], None, ALU.mult)
            for b in range(0, B, 4):
                dve.tensor_tensor(at_place[:, b:b + 4, :], slot_lo[:, b:b + 4].unsqueeze(2).to_broadcast([P, 4, P]),
                                  places[:, :].unsqueeze(1).to_broadcast([P, 4, P]), ALU.is_equal).then_inc(places_ready, 1)
            dve.wait_ge(table_in_psum, 1)
            dve.tensor_reduce(table_cols[:, :], banks[5][:, 0:2 * NTILE].rearrange("p (n t) -> p t n", n=2), AX.X, ALU.add
                              ).then_inc(table_ready, 1)

            for t in (wq_pad, wq2_pad, wk2_pad):
                dve.memset(t[:, :, :], 0.0)
            for t in (w1_pad, w2_pad):
                ins = dve.memset(t[:, :, DFF:DFFP], 0.0)
            ins.then_inc(dve_const, 1)
            dve.wait_ge(dve_const, 2)

            def copy_tiles(i):
                for j in range(UN):
                    dve.wait_ge(kv_in_psum[j], i + 1)
                    at_least(dve, kv_stored[j], 16 * i)
                    dve.tensor_copy(tile_kv[j][:, :], banks[2 + j][:, :]).then_inc(kv_copied[j], 1)

            copy_tiles(0)
            with dve.Fori(1, TURNS - 2) as i:
                copy_tiles(i)

            dve.wait_ge(weights_loaded, 16 * 4)
            dve.wait_ge(small_loaded, 16 * 8)

            def padded(t, k):
                return t[:, k, :].rearrange("p (h w) -> p h w", h=H)[:, :, 0:HD]

            def heads(t):
                return t.rearrange("p (h d) -> p h d", h=H)

            def prepare(k):
                dve.tensor_copy(padded(wq_pad, k), heads(raw_q[:, k, :]))
                dve.tensor_scalar(padded(wq2_pad, k), heads(raw_qkv[:, k, 0:D]), g1_col[:, k:k + 1], None, ALU.mult)
                dve.tensor_scalar(padded(wk2_pad, k), heads(raw_qkv[:, k, D:2 * D]), g1_col[:, k:k + 1], None, ALU.mult)
                dve.tensor_scalar(wv2[:, k, :], raw_qkv[:, k, 2 * D:3 * D], g1_col[:, k:k + 1], None, ALU.mult)
                dve.tensor_scalar(w1_pad[:, k, 0:DFF], w1_pad[:, k, 0:DFF], g2_col[:, k:k + 1], None, ALU.mult)
                dve.tensor_scalar(w2_pad[:, k, 0:DFF], w2_pad[:, k, 0:DFF], g2_col[:, k:k + 1], None, ALU.mult
                                  ).then_inc(prepared, 1)

            prepare(0)
            dve.wait_ge(rows_loaded, 32)
            dve.tensor_scalar(open_rows[:, :], pad_rows[:, :], -NEG, NEG, ALU.mult, ALU.add)
            dve.tensor_scalar(open_cols[:, :], pad_cols[:, :], -NEG, NEG, ALU.mult, ALU.add).then_inc(prepared, 1)
            copy_tiles(TURNS - 2)
            prepare(1)
            dve.wait_ge(prepared, KC + 1)

            F_STEPS, X_STEPS, Y_STEPS, Z_STEPS = 6, 9, 8, 2
            ROW_STEPS = F_STEPS + X_STEPS + Y_STEPS + Z_STEPS
            base, count = [0] * NS, [0] * NS

            def step(s, ins):
                count[s] += 1
                ins.then_inc(dve_step[s], 1)

            def last_step(s):
                dve.wait_ge(dve_step[s], base[s] + count[s])

            def moments(s, src):
                step(s, dve.bn_stats(stats[s][:, :], src))
                last_step(s)
                dve.memset(dve_held[:, :], 0.0)
                step(s, dve.bn_aggr(mean_var[s][:, :], stats[s][:, :]))
                last_step(s)
                step(s, dve.tensor_scalar(pow_in[s][:, 0:1], mean_var[s][:, 1:2], LN_EPS, None, ALU.add))
                last_step(s)
                dve.scalar_tensor_tensor(pow_in[s][:, 1:2], pow_in[s][:, 0:1], RMS_EPS, mean_var[s][:, 1:2],
                                         ALU.mult, ALU.add).then_inc(pow_asked[s], 1)

            def time_masks(s, it):
                b = NS * it + s
                t_row = time_rows[:, bass.ds(b * P, P)]
                t_col = time_cols[:, bass.ds(b, 1)]
                step(s, dve.scalar_tensor_tensor(neg_l[s][:, :], t_row, t_col, open_rows[:, bass.ds(b * P, P)],
                                                 ALU.is_le, ALU.mult))
                dve.tensor_scalar(neg_t[s][:, :], t_row, t_col, open_cols[:, bass.ds(b, 1)], ALU.is_ge, ALU.mult
                                  ).then_inc(masks_ready[s], 1)
                last_step(s)
                step(s, dve.tensor_reduce(any_open[s][:, :], neg_l[s][:, :], AX.X, ALU.max))

            def normalise_x(s, it):
                dve.wait_ge(pow_ready[s], 3 * it + 1)
                last_step(s)
                step(s, dve.scalar_tensor_tensor(q_rstd[s][:, :], any_open[s][:, :], 0.0, pow_out[s][:, 0:1],
                                                 ALU.is_equal, ALU.mult))
                last_step(s)
                dve.tensor_scalar(xn[s][:, :], x_sb[s][:, :], mean_var[s][:, 0:1], q_rstd[s][:, 0:1],
                                  ALU.subtract, ALU.mult).then_inc(xn_ready[s], 1)

            def maxima(s, u):
                dve.wait_ge(scores_ready[s], u + 1)
                for g in range(G):
                    ins = dve.tensor_reduce(max_pad[s][:, :, g, HD], bank(s, g)[:, :].rearrange("p (c m) -> p c m", c=C),
                                            AX.X, ALU.max)
                ins.then_inc(max_ready[s], 1)

            def join_max(s, u):
                dve.wait_ge(max_in_psum[s], u + 1)
                dve.tensor_tensor(q_aug[s][:, :, :], bank(s, 0)[:, :].rearrange("p (c m) -> p c m", c=C), q_t[s][:, :, :],
                                  ALU.add).then_inc(q_aug_ready[s], 1)

            def divide(s, u):
                dve.wait_ge(pv_ready[s], u + 1)
                step(s, dve.transpose(mixed_blocks[s][:, :, :].rearrange("p h w -> p (h w)"), bank(s, 0)[:, :]))
                last_step(s)
                step(s, dve.reciprocal(denom[s][:, :].unsqueeze(2), mixed_blocks[s][:, :, HD:HD + 1]))
                last_step(s)
                for k in range(KC):
                    eight = slice(H // 2 * k, H // 2 * (k + 1))
                    ins = dve.tensor_tensor(attn_blocks[s][:, k, :, :, :].rearrange("p l r j -> p r l j"),
                                            mixed_blocks[s][:, eight, 0:HD].rearrange("p (r l) j -> p r l j", r=2),
                                            denom[s][:, eight].rearrange("p (r l) -> p r l", r=2).unsqueeze(3)
                                            .to_broadcast([P, 2, G, HD]), ALU.mult)
                step(s, ins)
                last_step(s)
                for k in range(KC):
                    dve.transpose(attn_t[s][:, k, :], attn_blocks[s][:, k, :, :, :].rearrange("p l r j -> p (l r j)")
                                  ).then_inc(attn_t_ready[s], 1)

            def residual1(s, it):
                dve.wait_ge(mixed_ready[s], 2 * it + 1)
                dve.wait_ge(x_bias_ready[s], it + 1)
                at_least(dve, out_ready[s], it)
                step(s, dve.scalar_tensor_tensor(x1[s][:, :], bank(s, 2)[:, 0:D], gates[:, 0:1], x_bias[s][:, :],
                                                 ALU.mult, ALU.add))
                last_step(s)
                dve.memset(dve_held[:, :], 0.0).then_inc(x1_ready[s], 1)

            def normalise_x1(s, it):
                dve.wait_ge(pow_ready[s], 3 * it + 2)
                dve.tensor_scalar(h[s][:, :], x1[s][:, :], mean_var[s][:, 0:1], pow_out[s][:, 1:2],
                                  ALU.subtract, ALU.mult).then_inc(h_ready[s], 1)
                step(s, dve.tensor_scalar(y[s][:, :], x1[s][:, :], mean_var[s][:, 0:1], pow_out[s][:, 0:1],
                                          ALU.subtract, ALU.mult))
                last_step(s)
                step(s, dve.tensor_tensor_reduce(junk[s][:, :], y[s][:, :], router_row[:, :], 1.0, 0.0, ALU.mult,
                                                 ALU.add, score[s][:, 0:1]))
                last_step(s)
                dve.tensor_copy(score_wide[s][:, :], score[s][:, 0:1].to_broadcast([P, P])).then_inc(score_ready[s], 1)

            def rank_masks(s, it):
                dve.wait_ge(score_in_psum[s], it + 1)
                row, col = bank(s, 0)[:, 0:P], score[s][:, 0:1]
                dve.scalar_tensor_tensor(mask_a[s][:, :], row, col, later_neg[:, :], ALU.is_le, ALU.mult)
                step(s, dve.tensor_scalar(mask_b[s][:, :], row, col, NEG, ALU.is_lt, ALU.mult))
                last_step(s)
                step(s, dve.tensor_tensor(neg_l[s][:, :], mask_a[s][:, :], mask_b[s][:, :], ALU.min))
                last_step(s)
                dve.scalar_tensor_tensor(mask_a[s][:, :], row, col, earlier_neg[:, :], ALU.is_ge, ALU.mult)
                step(s, dve.tensor_scalar(mask_b[s][:, :], row, col, NEG, ALU.is_gt, ALU.mult))
                last_step(s)
                dve.tensor_tensor(neg_t[s][:, :], mask_a[s][:, :], mask_b[s][:, :], ALU.min).then_inc(masks_ready[s], 1)

            def residual2(s, it):
                dve.wait_ge(mixed_ready[s], 2 * it + 2)
                step(s, dve.tensor_tensor(x2[s][:, :], bank(s, 2)[:, 0:D], y[s][:, :], ALU.add))
                last_step(s)
                step(s, dve.tensor_tensor_reduce(junk[s][:, :], x2[s][:, :], x2[s][:, :], 1.0 / D, 0.0, ALU.mult,
                                                 ALU.add, score[s][:, 0:1]))
                last_step(s)
                dve.tensor_scalar(pow_in[s][:, :], score[s][:, 0:1].to_broadcast([P, 2]), RMS_EPS, None, ALU.add
                                  ).then_inc(pow_asked[s], 1)

            def normalise_x2(s, it):
                dve.wait_ge(pow_ready[s], 3 * it + 3)
                dve.tensor_scalar(h2[s][:, :], x2[s][:, :], pow_out[s][:, 0:1], None, ALU.mult).then_inc(h2_ready[s], 1)

            def swiglu(s, it):
                dve.wait_ge(tanh_ready[s], it + 1)
                dve.scalar_tensor_tensor(silu_a[s][:, 0:512], tanh_a[s][:, 0:512], 1.0, bank(s, 1)[:, :], ALU.add, ALU.mult)
                step(s, dve.scalar_tensor_tensor(silu_a[s][:, 512:DFFP], tanh_a[s][:, 512:DFFP], 1.0,
                                                 bank(s, 2)[:, 0:DFFP - 512], ALU.add, ALU.mult))
                dve.wait_ge(ff_b_ready[s], it + 1)
                last_step(s)
                dve.scalar_tensor_tensor(hidden[s][:, 0:512], bank(s, 3)[:, :], 0.5, silu_a[s][:, 0:512], ALU.mult, ALU.mult)
                dve.scalar_tensor_tensor(hidden[s][:, 512:DFFP], bank(s, 0)[:, 0:DFFP - 512], 0.5, silu_a[s][:, 512:DFFP],
                                         ALU.mult, ALU.mult).then_inc(hidden_ready[s], 1)

            def residual3_first(s, it):
                dve.wait_ge(ff_first_ready[s], it + 1)
                dve.tensor_tensor(x3[s][:, :], bank(s, 3)[:, 0:D], x2[s][:, :], ALU.add).then_inc(x3_ready[s], 1)

            def residual3(s, it, rest):
                dve.wait_ge(ff_ready[s], it + 1)
                dve.wait_ge(x3_ready[s], it + 1)
                step(s, dve.tensor_tensor(x4[s][:, :], rest[:, 0:D], x3[s][:, :], ALU.add))
                at_least(dve, out_stored[s], 16 * it)
                last_step(s)
                dve.scalar_tensor_tensor(y_out[s][:, :], x4[s][:, :], gates[:, 1:2], x1[s][:, :], ALU.mult, ALU.add
                                         ).then_inc(out_ready[s], 1)

            dve.wait_ge(consts_ready, 1)
            dve.wait_ge(pads_ready, 2 * NS)

            def half(it, s, has_x, y_it, has_z, f_it):
                t = 1 - s
                has_y, has_f = y_it is not None, f_it is not None
                if has_z:
                    swiglu(s, it - 1)
                if has_y:
                    rank_masks(t, y_it)
                if has_z:
                    residual3_first(s, it - 1)
                if has_y:
                    maxima(t, 2 * y_it + 1)
                    join_max(t, 2 * y_it + 1)
                if has_x:
                    maxima(s, 2 * it)
                    join_max(s, 2 * it)
                if has_y:
                    divide(t, 2 * y_it + 1)
                    residual2(t, y_it)
                if has_f:
                    time_masks(t, f_it)
                if has_y:
                    normalise_x2(t, y_it)
                if has_x:
                    divide(s, 2 * it)
                if has_z:
                    residual3(s, it - 1, bank(t, 3) if has_x else bank(s, 2))
                if has_f:
                    dve.wait_ge(x_loaded[t], 16 * f_it + 16)
                    moments(t, x_sb[t][:, :])
                if has_x:
                    residual1(s, it)
                    moments(s, x1[s][:, :])
                if has_f:
                    normalise_x(t, f_it)
                if has_x:
                    normalise_x1(s, it)

            def rows(it, first=False, left=1):
                if not first:
                    base[0] = ROW_STEPS * it - Z_STEPS + (F_STEPS if left >= 0 else 0)
                    base[1] = ROW_STEPS * it - Y_STEPS - Z_STEPS
                    count[:] = [0, 0]
                half(it, 0, left >= 0, None if first else it - 1, not first, it if left >= 0 else None)
                if left >= 0:
                    half(it, 1, True, it, not first, it + 1 if left >= 1 else None)
                    assert count[0] == ROW_STEPS + first * (F_STEPS - Z_STEPS) - (left < 1) * F_STEPS, count
                    assert count[1] == (F_STEPS + X_STEPS if first else ROW_STEPS), count

            time_masks(0, 0)
            dve.wait_ge(x_loaded[0], 16)
            moments(0, x_sb[0][:, :])
            copy_tiles(TURNS - 1)
            dve.wait_ge(last_loaded, 16 * 4)
            dve.wait_ge(gates_ready, 1)
            dve.tensor_scalar(bias_row[:, :], bias_row[:, :], gates[:, 0:1], None, ALU.mult).then_inc(weights_ready, 1)
            normalise_x(0, 0)
            rows(0, first=True)
            with dve.Fori(1, NB - 1) as it:
                rows(it)
            rows(NB - 1, left=0)
            rows(NB, left=-1)
            swiglu(1, NB - 1)
            residual3_first(1, NB - 1)
            residual3(1, NB - 1, bank(0, 3))


_ORDER = ["x", "ctx", "times", "times_t", "bucket_t", "pad", "pad_t", "g_x", "g_f", "wq", "wkv", "wo", "bo",
          "w_router", "wqkv_t", "wout_t", "g1", "g2", "w1t", "w2t", "w3t"]


def kernel(x, ctx_1024, fside_BxS2_0, itok_BxS2_0_7, mask_BxS2_bf0, g_xattn, g_ffn, L0_xattn_Wq, L0_xattn_Wk_b,
           L0_xattn_Wv_b, L0_xattn_Wo, L0_xattn_bo, L0_ffn_w_router, L0_ffn_W_qkv, L0_ffn_W_out, L0_ffn_g1,
           L0_ffn_g2, L0_ffn_W1, L0_ffn_W2, L0_ffn_W3):
    import concourse.bacc as bacc
    from concourse.bass_utils import run_bass_kernel_spmd

    lay = lambda a: np.ascontiguousarray(a)

    def mixing_rows(w):
        return lay(np.asarray(w).reshape(KC, 2, G, HD, D).transpose(2, 1, 3, 0, 4).reshape(P, KC * D))

    wkv = np.concatenate([np.asarray(L0_xattn_Wk_b), np.asarray(L0_xattn_Wv_b)], axis=-1)
    wkv = wkv.reshape(E, KC, P, 2 * D).transpose(2, 1, 0, 3).reshape(P, KC * E * 2 * D)
    pad = lay(mask_BxS2_bf0)
    data = {
        "x": lay(x), "ctx": lay(ctx_1024).reshape(B * P, D), "times": lay(fside_BxS2_0),
        "times_t": lay(np.asarray(fside_BxS2_0).T), "bucket_t": lay(np.asarray(itok_BxS2_0_7).T),
        "pad": pad, "pad_t": lay(pad.T), "g_x": lay(g_xattn), "g_f": lay(g_ffn), "wq": lay(L0_xattn_Wq),
        "wkv": lay(wkv), "wo": mixing_rows(L0_xattn_Wo), "bo": lay(L0_xattn_bo), "w_router": lay(L0_ffn_w_router),
        "wqkv_t": lay(np.asarray(L0_ffn_W_qkv).T), "wout_t": mixing_rows(np.asarray(L0_ffn_W_out).T),
        "g1": lay(np.asarray(L0_ffn_g1).reshape(KC, P).T), "g2": lay(np.asarray(L0_ffn_g2).reshape(KC, P).T),
        "w1t": lay(np.asarray(L0_ffn_W1).T),
        "w2t": lay(np.asarray(L0_ffn_W2).T), "w3t": lay(np.asarray(L0_ffn_W3).T),
    }
    nc = bacc.Bacc("TRN2", target_bir_lowering=False, num_devices=1)
    arrays, args = {}, []
    for name in _ORDER:
        arrays[f"in_{name}"] = data[name]
        args.append(nc.dram_tensor(f"in_{name}", data[name].shape, mybir.dt.from_np(data[name].dtype),
                                   kind="ExternalInput").ap())
    args.append(nc.dram_tensor("out_0", (B, P, D), F32, kind="ExternalOutput").ap())
    build(nc, *args)
    r = run_bass_kernel_spmd(nc, [arrays], core_ids=[0])
    return r.results[0]["out_0"]
```
